# Optimizing a Trainium2 kernel written in Bass

```python
import numpy as np
import jax
import jax.numpy as jnp

def _softmax(x, axis=-1):
    return jax.nn.softmax(x, axis=axis)

def _gelu(x):
    return jax.nn.gelu(x, approximate=True)

def _silu(x):
    return jax.nn.silu(x)

def _sigmoid(x):
    return jax.nn.sigmoid(x)

def _layernorm(x, axis=-1, eps=1e-05):
    m = jnp.mean(x, axis=axis, keepdims=True)
    v = jnp.var(x, axis=axis, keepdims=True)
    return (x - m) / jnp.sqrt(v + eps)

def _scatter_add(tgt, idx, src, axis=0):
    return tgt.at[idx].add(src)

def _segment_sum(src, seg, n):
    return jax.ops.segment_sum(src, seg, n)
kernel_name = 'mk_macaron_d1_jaxref_r8_bf0d4b'

def setup_inputs(seed: int=0):
    np.random.seed(seed)
    _w = jnp.asarray

    def _L0_attn_setup():
        import jax, jax.numpy as jnp
        import numpy as np
        DIM = 128
        HEADS = 16
        HEAD_DIM = 64
        WINDOW = 64
        key = jax.random.key(seed)
        ks = jax.random.split(key, 9)
        s = lambda fan_in: 1.0 / np.sqrt(fan_in)
        x = jax.random.normal(ks[0], (2, 256, DIM), dtype=jnp.float32)
        W1 = jax.random.uniform(ks[1], (DIM, DIM), jnp.float32, -s(DIM), s(DIM))
        b1 = jax.random.uniform(ks[2], (DIM,), jnp.float32, -s(DIM), s(DIM))
        W2 = jax.random.uniform(ks[3], (DIM, DIM), jnp.float32, -s(DIM), s(DIM))
        b2 = jax.random.uniform(ks[4], (DIM,), jnp.float32, -s(DIM), s(DIM))
        Wg = jax.random.uniform(ks[5], (3 * HEADS * HEAD_DIM, DIM), jnp.float32, -s(DIM), s(DIM))
        bg = jax.random.uniform(ks[6], (3 * HEADS * HEAD_DIM,), jnp.float32, -s(DIM), s(DIM))
        Wo = jax.random.uniform(ks[7], (DIM, HEADS * HEAD_DIM), jnp.float32, -s(HEADS * HEAD_DIM), s(HEADS * HEAD_DIM))
        bo = jax.random.uniform(ks[8], (DIM,), jnp.float32, -s(HEADS * HEAD_DIM), s(HEADS * HEAD_DIM))
        return {'x': x, 'W1': W1, 'b1': b1, 'W2': W2, 'b2': b2, 'Wg': Wg, 'bg': bg, 'Wo': Wo, 'bo': bo}
    _L0_attn_in = _L0_attn_setup()

    def _L0_ffn_setup():
        import jax, jax.numpy as jnp
        import numpy as np
        DIM = 128
        HIDDEN = 384
        SCALE = 1.0 / 127.0

        def _dequant(w_int, dtype):
            return w_int.astype(dtype) * jnp.asarray(SCALE, dtype)
        key = jax.random.key(seed)
        k_x, k_g, k_u, k_d = jax.random.split(key, 4)
        x = jax.random.normal(k_x, (4, 256, DIM), dtype=jnp.float32)
        w_gate = jax.random.randint(k_g, (HIDDEN, DIM), -127, 128, dtype=jnp.int32)
        w_up = jax.random.randint(k_u, (HIDDEN, DIM), -127, 128, dtype=jnp.int32)
        w_down = jax.random.randint(k_d, (DIM, HIDDEN), -127, 128, dtype=jnp.int32)
        return {'x': x, 'w_gate': w_gate, 'w_up': w_up, 'w_down': w_down}
    _L0_ffn_in = _L0_ffn_setup()
    _d = {'L0_attn_x': _L0_attn_in['x'], 'L0_attn_W1': _L0_attn_in['W1'], 'L0_attn_b1': _L0_attn_in['b1'], 'L0_attn_W2': _L0_attn_in['W2'], 'L0_attn_b2': _L0_attn_in['b2'], 'L0_attn_Wg': _L0_attn_in['Wg'], 'L0_attn_bg': _L0_attn_in['bg'], 'L0_attn_Wo': _L0_attn_in['Wo'], 'L0_attn_bo': _L0_attn_in['bo'], 'L0_ffn_w_gate': _L0_ffn_in['w_gate'], 'L0_ffn_w_up': _L0_ffn_in['w_up'], 'L0_ffn_w_down': _L0_ffn_in['w_down']}
    _x0 = _d['L0_attn_x']
    _d['L0_attn_x'] = jax.random.normal(jax.random.fold_in(jax.random.key(seed), 1), (4, 1024, 128), dtype=_x0.dtype)
    del _x0
    return _d

def reference(L0_attn_x, L0_attn_W1, L0_attn_b1, L0_attn_W2, L0_attn_b2, L0_attn_Wg, L0_attn_bg, L0_attn_Wo, L0_attn_bo, L0_ffn_w_gate, L0_ffn_w_up, L0_ffn_w_down):

    def _L0_attn_ref(x, W1, b1, W2, b2, Wg, bg, Wo, bo):
        import jax, jax.numpy as jnp
        import numpy as np
        DIM = 128
        HEADS = 16
        HEAD_DIM = 64
        WINDOW = 64
        b, n, _ = x.shape
        h = jax.nn.silu(x @ W1.T + b1) @ W2.T + b2
        qkv = h @ Wg.T + bg
        q, k, v = jnp.split(qkv, 3, axis=-1)
        reshape = lambda t: t.reshape(b, n, HEADS, HEAD_DIM).transpose(0, 2, 1, 3)
        q, k, v = (reshape(q), reshape(k), reshape(v))
        dots = jnp.einsum('bhid,bhjd->bhij', q, k) * HEAD_DIM ** (-0.5)
        i = jnp.arange(n)[:, None]
        j = jnp.arange(n)[None, :]
        mask = j >= i + WINDOW
        dots = jnp.where(mask, -jnp.inf, dots)
        attn = jax.nn.softmax(dots, axis=-1)
        out = jnp.einsum('bhij,bhjd->bhid', attn, v)
        out = out.transpose(0, 2, 1, 3).reshape(b, n, HEADS * HEAD_DIM)
        return out @ Wo.T + bo

    def _L0_ffn_ref(x, w_gate, w_up, w_down):
        import jax, jax.numpy as jnp
        import numpy as np
        DIM = 128
        HIDDEN = 384
        SCALE = 1.0 / 127.0

        def _dequant(w_int, dtype):
            return w_int.astype(dtype) * jnp.asarray(SCALE, dtype)
        wg = _dequant(w_gate, x.dtype)
        wu = _dequant(w_up, x.dtype)
        wd = _dequant(w_down, x.dtype)
        gate = jnp.einsum('bsd,hd->bsh', x, wg)
        up = jnp.einsum('bsd,hd->bsh', x, wu)
        h = jax.nn.silu(gate) * up
        return jnp.einsum('bsh,dh->bsd', h, wd)
    x = L0_attn_x
    x = x + 0.5 * _L0_ffn_ref(_layernorm(x, axis=-1), L0_ffn_w_gate, L0_ffn_w_up, L0_ffn_w_down)
    x = x + _L0_attn_ref(_layernorm(x, axis=-1), L0_attn_W1, L0_attn_b1, L0_attn_W2, L0_attn_b2, L0_attn_Wg, L0_attn_bg, L0_attn_Wo, L0_attn_bo)
    x = x + 0.5 * _L0_ffn_ref(_layernorm(x, axis=-1), L0_ffn_w_gate, L0_ffn_w_up, L0_ffn_w_down)
    return x

_drawn_inputs = setup_inputs


def setup_inputs(seed=0):
    import zlib

    import numpy as np

    out = dict(_drawn_inputs(seed))
    spreads = {}
    factors = {'L0_attn_W1': 8.0,
     'L0_attn_b1': 8.0,
     'L0_attn_W2': 8.0,
     'L0_attn_b2': 8.0,
     'L0_attn_Wg': 8.0,
     'L0_attn_bg': 8.0,
     'L0_attn_Wo': 8.0,
     'L0_attn_bo': 8.0}
    for name, (base, spread) in spreads.items():
        noise = np.random.default_rng([zlib.crc32(name.encode()), seed]).standard_normal(out[name].shape)
        drawn = base * np.exp(spread * noise) if base else spread * noise
        out[name] = jnp.asarray(drawn.astype(out[name].dtype))
    for name, factor in factors.items():
        out[name] = (out[name] * factor).astype(out[name].dtype)
    return out
```

```python
from contextlib import ExitStack

import concourse.bass as bass
from concourse import mybir

F32 = mybir.dt.float32
F32R = mybir.dt.float32r
BF16 = mybir.dt.bfloat16
I32 = mybir.dt.int32
ALU = mybir.AluOpType
ACT = mybir.ActivationFunctionType
AX = mybir.AxisListType
MAX = bass.bass_isa.ReduceOp.max

P = 128
BANK = 512
MASKED = -3.0e38
EPS = 1e-5


class Tally:

    def __init__(self, sem, events, step=1):
        self.sem, self.events, self.step = sem, list(events), step
        self.per_pass = len(self.events) * step

    def after(self, event, turn):
        return (turn + 1) * self.per_pass + (self.events.index(event) + 1) * self.step

    def before(self, event, turn):
        return turn * self.per_pass + (self.events.index(event) + 1) * self.step


def macaron(nc, x, w1t, b1, w2t, b2, wqkvt, bqk, bv, wot, bo, wgatet, wupt, wdownt, out):
    TOK, D = x.shape
    BATCH, N = 4, TOK // 4
    DH, WINDOW = 64, 64
    PAIRS = wot.shape[0] // P
    TURNS = BATCH * PAIRS
    HID = wgatet.shape[1]
    HB = HID // P
    FS = 1.0 / 127.0
    CH = 512
    CHUNKS = TOK // CH
    CT = CH // P
    QC = 256
    assert D == P and N == 1024 and CH == BANK

    UNITS = [(3, 0), (1, 0), (3, 1), (1, 1), (2, 0), (2, 1), (0, 0), (0, 1)]
    RING = {(3, 0): 0, (1, 0): 4, (3, 1): 0, (1, 1): 4, (2, 0): 0, (2, 1): 3, (0, 0): 0, (0, 1): 1}
    WORK, ATTN = 7, 6

    def pieces(c):
        full = [(kb, kb * QC, QC, 0) for kb in range(2 * c + 1)]
        part = [(2 * c + 1, (2 * c + 1) * QC, QC - WINDOW, WINDOW)]
        last = [(2 * c + 2, (2 * c + 2) * QC - WINDOW, WINDOW, QC - WINDOW)] if 2 * c + 2 < N // P else []
        return full + part + last

    def width(c):
        return sum(w for _, _, w, _ in pieces(c))

    def parts(c):
        return [(b, min(b + 2, c + 1)) for b in range(0, c + 1, 2)]

    def unit(u):
        return f"{u[0]}{'AB'[u[1]]}"

    with ExitStack() as ctx:
        def sb(name, shape, dt=F32):
            return ctx.enter_context(nc.sbuf_tensor(name, shape, dt))

        def sem(name):
            return ctx.enter_context(nc.semaphore(name))

        ident = sb("ident", [P, P])
        ident16 = sb("ident16", [P, P], BF16)
        mask16 = sb("mask16", [P, P], BF16)
        ones64 = sb("ones64", [P, DH])
        minus1 = sb("minus1", [P, P], F32R)
        w1_sb = sb("w1_sb", [P, P])
        w2_sb = sb("w2_sb", [P, P])
        b1_sb = sb("b1_sb", [P, 1])
        b2_sb = sb("b2_sb", [P, 1])
        bqk_sb = sb("bqk_sb", [P, PAIRS, 2])
        bv_sb = sb("bv_sb", [P, PAIRS])
        bvx = sb("bvx", [P, PAIRS, P])
        bo_row = sb("bo_row", [1, P])
        ones_row = sb("ones_row", [1, P])
        bo_all = sb("bo_all", [P, P])
        wo_sb = sb("wo_sb", [P, PAIRS, P])
        wff = sb("wff", [P, 2 * HB, P], F32R)
        wdn = sb("wdn", [P, HB, P])
        xres = sb("xres", [P, TOK // P * D])
        probs = {(c, h): sb(f"probs{c}{h}", [P, (c + 1) * BANK]) for c in range(4) for h in range(2)}
        blockmax = {u: sb(f"blockmax{unit(u)}", [P, QC]) for u in UNITS}
        rowmax = {u: sb(f"rowmax{unit(u)}", [P, QC]) for u in UNITS}
        maxrows = {u: sb(f"maxrows{unit(u)}", [P, QC], F32R) for u in UNITS}
        keysum = {u: sb(f"keysum{unit(u)}", [P, QC]) for u in UNITS}
        qs = [[sb(f"qs{r}{h}", [P, N], F32R) for h in range(2)] for r in range(2)]
        ks = [[sb(f"ks{r}{h}", [P, 2, N], F32R) for h in range(2)] for r in range(2)]
        vs = [sb(f"vs{r}", [P, N // P, P]) for r in range(2)]
        attn = sb("attn", [P, N])
        rsum = sb("rsum", [P, QC])
        hb = sb("hb", [P, 2, N], F32R)
        wslot = sb("wslot", [P, 3, 2, P], F32R)
        bslot = sb("bslot", [P, 2])
        xin = [sb(f"xin{r}", [P, CT, D]) for r in range(2)]
        xn = sb("xn", [P, CT, D])
        x1 = sb("x1", [P, CT, D])
        x1b = sb("x1b", [P, CT, D])
        stats = sb("stats", [P, CT, 6])
        mv = sb("mv", [P, CT, 2])
        rstd = sb("rstd", [P, CT])
        veps = sb("veps", [P, CT])
        mhalf = sb("mhalf", [P, CT])
        xth = sb("xth", [P, 2, CH], F32R)
        gated = probs[3, 0][:, 0:HB * CH].rearrange("p (j n) -> p j n", j=HB)
        hidden = probs[3, 1][:, 0:HB * CH].rearrange("p (j n) -> p j n", j=HB)
        x2t = probs[2, 0][:, 0:CH]
        y1 = probs[2, 1][:, 0:CH]
        hch = sb("hch", [P, 2, CH], F32R)
        iload = sb("iload", [P, 3 * HID], I32)
        wload = probs[2, 0][:, 0:3 * P].rearrange("p (t n) -> p t n", t=3)
        wsplit = sb("wsplit", [P, 3, 2, P], F32R)

        banks = ctx.enter_context(nc.psum_tensor("banks", [P, 8, BANK], F32))

        h_dram = nc.dram_tensor("h_scratch", [2, P, TOK], F32, kind="Internal").ap()
        w_dram = nc.dram_tensor("w_scratch", [P, PAIRS, 3 * 2 * P], F32, kind="Internal").ap()

        loaded = sem("loaded")
        consts = sem("consts")
        gp_const = sem("gp_const")
        bvx_ready = sem("bvx_ready")
        bo_done = sem("bo_done")
        w_in = sem("w_in")
        w_hi = sem("w_hi")
        w_lo = sem("w_lo")
        w_out = sem("w_out")
        idle = sem("idle")

        class Phase:
            pass

        def phase(name, first):
            t = Phase()
            t.first = first
            two = ["ln1", "ln2"] if first else ["ln1"]
            T = lambda n, ev, step=1: Tally(sem(f"{name}_{n}"), ev, step)
            t.xin = T("xin", ["x"], 16)
            t.stat = T("stat", [f"{l}{k}{s}" for l in two for s in "sa" for k in range(CT)])
            t.rstd = T("rstd", [e for l in two for e in (l + "e", l)])
            t.norm = T("norm", two)
            t.tr = T("tr", two)
            t.xhi = T("xhi", two)
            t.xlo = T("xlo", ["ln1"])
            t.gu = T("gu", [f"g{j}" for j in range(HB)] + [f"u{j}" for j in range(HB)])
            t.silu = T("silu", [f"g{j}" for j in range(HB)])
            t.hid = T("hid", [f"h{j}" for j in range(HB)])
            t.down = T("down", ["d"])
            t.x1 = T("x1", ["x1"])
            t.x1b = T("x1b", ["x1b"])
            t.store = T("store", ["s"], 16)
            t.m1 = T("m1", ["m1"])
            t.y1 = T("y1", ["y1"])
            t.m2 = T("m2", ["m2"])
            t.hhi = T("hhi", ["h"])
            t.hlo = T("hlo", ["h"])
            t.hstore = T("hstore", ["h"], 16)
            return t

        pa, pd = phase("a", True), phase("d", False)

        T = lambda n, ev, step=1: Tally(sem(n), ev, step)
        HALVES = ["q0", "q1", "k0", "k1"]
        score_events = [e for u in UNITS for e in ([unit(u) + "a"] if u[0] else []) + [unit(u) + "b"]]
        piece_events = [f"{unit(u)}.{n}" for u in UNITS for n in range(len(parts(u[0])))]
        scores = T("scores", score_events)
        maxed = T("maxed", [unit(u) for u in UNITS])
        gmax = T("gmax", [unit(u) for u in UNITS])
        rows = T("rows", [unit(u) for u in UNITS])
        shifted = T("shifted", piece_events)
        exped = T("exped", piece_events)
        DVE_SUMS = [(3, 0), (3, 1)]
        POOL_SUMS = [(1, 0), (1, 1), (2, 0), (2, 1), (0, 0), (0, 1)]
        dsum = T("dsum", [unit(u) for u in DVE_SUMS])
        psum = T("psum_", [unit(u) for u in POOL_SUMS])
        CORDER = [3, 1, 2, 0]
        pv = T("pv", [f"c{c}" for c in CORDER])
        normed = T("normed", [f"c{c}" for c in CORDER])
        proj = T("proj", HALVES + ["v0", "v1"])
        hi_done = T("hi_done", HALVES)
        lo_done = T("lo_done", HALVES)
        v_done = T("v_done", ["v0", "v1"])
        kdup = T("kdup", ["A", "B"], 16)
        slots = T("slots", ["h", "w", "b"], 16)
        wo_done = T("wo_done", ["o0", "o1"])
        wo_added = T("wo_added", ["o0", "o1"])
        dve_step = T("dve_step", range(34))
        pool_step = T("pool_step", range(20))

        credits = {
            "sync": [kdup, slots], "vector": [maxed, rows, dsum, normed, lo_done, wo_added, dve_step],
            "scalar": [exped, hi_done, v_done], "tensor": [scores, shifted, pv, proj, wo_done],
            "gpsimd": [gmax, psum, pool_step],
        }
        for t in (pa, pd):
            credits["sync"] += [t.xin, t.store, t.hstore]
            credits["vector"] += [t.stat, t.norm, t.xlo, t.hid, t.x1, t.hlo]
            credits["gpsimd"] += [t.rstd, t.x1b]
            credits["tensor"] += [t.tr, t.gu, t.down, t.m1, t.m2]
            credits["scalar"] += [t.xhi, t.silu, t.y1, t.hhi]

        def give_credits(eng, name):
            for t in credits[name]:
                eng.sem_inc(t.sem, t.per_pass)

        def after(eng, tally, event, turn):
            eng.wait_ge(tally.sem, tally.after(event, turn))

        def before(eng, tally, event, turn):
            eng.wait_ge(tally.sem, tally.before(event, turn))

        class Steps:

            def __init__(self, eng, tally):
                self.eng, self.tally = eng, tally

            def begin(self, turn):
                self.turn, self.n = turn, 0

            def mark(self, instruction):
                self.n += 1
                instruction.then_inc(self.tally.sem, 1)

            def wait(self):
                after(self.eng, self.tally, self.n - 1, self.turn)

            def end(self):
                assert self.n == len(self.tally.events), (self.n, len(self.tally.events))

        def half(h):
            return slice(DH * h, DH * h + DH)

        block = ctx.enter_context(nc.Block())

        @block.sync
        def _(sp):
            give_credits(sp, "sync")
            for dst, src in (
                (iload[:, 0:HID], wgatet), (iload[:, HID:2 * HID], wupt),
                (iload[:, 2 * HID:3 * HID].rearrange("p (j n) -> p j n", j=HB), wdownt.rearrange("(j p) n -> p j n", p=P)),
                (w1_sb[:], w1t), (w2_sb[:], w2t), (b1_sb[:], b1), (b2_sb[:], b2),
                (bqk_sb[:], bqk.rearrange("p (g t) -> p g t", t=2)), (bv_sb[:], bv),
                (wo_sb[:], wot.rearrange("(g p) n -> p g n", p=P)), (bo_row[:], bo),
            ):
                sp.dma_start(dst, src).then_inc(loaded, 16)
            wq_src = wqkvt.rearrange("p (t g n) -> p g t n", t=3, n=P)
            for g in range(PAIRS):
                if g:
                    sp.wait_ge(w_lo, g)
                sp.dma_start(wload, wq_src[:, g, :, :]).then_inc(w_in, 16)
                sp.wait_ge(w_hi, g + 1)
                sp.wait_ge(w_lo, g + 1)
                sp.dma_start(w_dram[:, g, :], wsplit[:].bitcast(F32).rearrange("p t s n -> p (t s n)")).then_inc(w_out, 16)
            sp.wait_ge(w_out, 16 * PAIRS)
            x_src = x.rearrange("(t k p) d -> p t k d", k=CT, p=P)
            with sp.Fori(0, CHUNKS // 2) as i:
                for r in range(2):
                    t = i * 2 + r
                    at = sp.snap(t * CH)
                    before(sp, pa.x1, "x1", t)
                    sp.dma_start(xin[r][:].unsqueeze(1), x_src[:, bass.ds(t, 1), :, :]).then_inc(pa.xin.sem, 16)
                    after(sp, pa.x1b, "x1b", t)
                    sp.dma_start(xres[:, bass.ds(at, CT * D)], x1b[:].rearrange("p k d -> p (k d)")).then_inc(pa.store.sem, 16)
                    after(sp, pa.hhi, "h", t)
                    after(sp, pa.hlo, "h", t)
                    sp.dma_start(h_dram[:, :, bass.ds(at, CH)].rearrange("s p n -> p s n"), hch[:].bitcast(F32)).then_inc(pa.hstore.sem, 16)
            after(sp, pa.store, "s", CHUNKS - 1)
            after(sp, pa.hstore, "h", CHUNKS - 1)

            with sp.Fori(0, TURNS // 2) as i:
                for r in range(2):
                    n = i * 2 + r
                    h_at = sp.snap((n // PAIRS) * N)
                    g_at = sp.snap(n % PAIRS)
                    before(sp, proj, "v1", n)
                    sp.dma_start(hb[:].bitcast(F32), h_dram[:, :, bass.ds(h_at, N)].rearrange("s p n -> p s n")).then_inc(slots.sem, 16)
                    sp.dma_start(wslot[:].bitcast(F32).rearrange("p t s n -> p (t s n)").unsqueeze(1), w_dram[:, bass.ds(g_at, 1), :]).then_inc(slots.sem, 16)
                    before(sp, lo_done, "k1", n)
                    sp.dma_start(bslot[:].unsqueeze(1), bqk_sb[:, bass.ds(g_at, 1), :]).then_inc(slots.sem, 16)
                    after(sp, hi_done, "k1", n)
                    after(sp, lo_done, "k1", n)
                    for h in range(2):
                        sp.dma_start(ks[r][h][half(1 - h)].bitcast(F32), ks[r][h][half(h)].bitcast(F32)).then_inc(kdup.sem, 16)

            after(sp, wo_added, "o1", TURNS - 1)
            out_dst = out.rearrange("(t k p) d -> p t k d", k=CT, p=P)
            with sp.Fori(0, CHUNKS // 2) as i:
                for r in range(2):
                    t = i * 2 + r
                    at = sp.snap(t * CH)
                    before(sp, pd.x1, "x1", t)
                    sp.dma_start(xin[r][:].rearrange("p k d -> p (k d)"), xres[:, bass.ds(at, CT * D)]).then_inc(pd.xin.sem, 16)
                    after(sp, pd.x1, "x1", t)
                    sp.dma_start(out_dst[:, bass.ds(t, 1), :, :], x1[:].unsqueeze(1)).then_inc(pd.store.sem, 16)
            sp.wait_ge(pd.store.sem, 16 * (CHUNKS + 1))

        @block.gpsimd
        def _(pool):
            give_credits(pool, "gpsimd")
            steps = Steps(pool, pool_step)
            nc.gpsimd.memset(ident[:], 0.0).then_inc(gp_const, 1)
            nc.gpsimd.memset(mask16[:], 0.0).then_inc(gp_const, 1)
            nc.gpsimd.memset(mhalf[:], -0.5).then_inc(gp_const, 1)
            pool.wait_ge(gp_const, 3)
            nc.gpsimd.affine_select(out=ident[:], in_=ident[:], compare_op=ALU.not_equal, fill=1.0, base=0,
                                    pattern=[[-1, P]], channel_multiplier=1).then_inc(gp_const, 1)
            nc.gpsimd.affine_select(out=mask16[:], in_=mask16[:], compare_op=ALU.is_ge, fill=MASKED, base=-1,
                                    pattern=[[1, P]], channel_multiplier=-1).then_inc(gp_const, 1)
            pool.wait_ge(gp_const, 5)
            nc.gpsimd.tensor_copy(ident16[:], ident[:]).then_inc(gp_const, 1)
            pool.wait_ge(gp_const, 6)

            def rstd_of(t, ln, turn):
                after(pool, t.stat, f"{ln}{CT - 1}a", turn)
                pool.sem_inc(idle, 1)
                nc.gpsimd.tensor_scalar(veps[:], mv[:, :, 1], EPS, None, ALU.add).then_inc(t.rstd.sem, 1)
                after(pool, t.rstd, f"{ln}e", turn)
                nc.gpsimd.tensor_tensor(rstd[:], veps[:], mhalf[:], ALU.pow).then_inc(t.rstd.sem, 1)

            pool.wait_ge(bo_done, 2)
            with pool.Fori(0, CHUNKS) as t:
                rstd_of(pa, "ln1", t)
                before(pool, pa.store, "s", t)
                after(pool, pa.x1, "x1", t)
                nc.gpsimd.tensor_tensor(x1b[:], x1[:], bo_all[:].unsqueeze(1).to_broadcast([P, CT, P]), ALU.add).then_inc(pa.x1b.sem, 1)
                rstd_of(pa, "ln2", t)

            def row_max(u, i):
                before(pool, rows, unit(u), i)
                after(pool, maxed, unit(u), i)
                pool.sem_inc(idle, 1)
                nc.gpsimd.partition_all_reduce(rowmax[u][:], blockmax[u][:], P, MAX).then_inc(gmax.sem, 1)

            def key_sum(u, i):
                c, pr, acc = u[0], probs[u], keysum[u]
                after(pool, exped, f"{unit(u)}.{len(parts(c)) - 1}", i)
                before(pool, pv, f"c{c}", i)
                if c == 0:
                    pool.sem_inc(idle, 1)
                    steps.mark(nc.gpsimd.tensor_copy(acc[:, 0:WINDOW], pr[:, 0:WINDOW]))
                rest = pieces(c)[1:]
                for n, (_, col, w, q0) in enumerate(rest):
                    if n:
                        steps.wait()
                    src = acc if n else pr
                    add = nc.gpsimd.tensor_tensor(acc[:, q0:q0 + w], src[:, q0:q0 + w], pr[:, col:col + w], ALU.add)
                    if n == len(rest) - 1:
                        add.then_inc(psum.sem, 1)
                    else:
                        steps.mark(add)

            with pool.Fori(0, TURNS) as i:
                steps.begin(i)
                row_max((3, 0), i)
                row_max((1, 0), i)
                key_sum((1, 0), i)
                row_max((3, 1), i)
                row_max((1, 1), i)
                key_sum((1, 1), i)
                row_max((2, 0), i)
                row_max((2, 1), i)
                row_max((0, 0), i)
                row_max((0, 1), i)
                key_sum((2, 0), i)
                key_sum((2, 1), i)
                key_sum((0, 0), i)
                key_sum((0, 1), i)
                steps.end()

            with pool.Fori(0, CHUNKS) as t:
                rstd_of(pd, "ln1", t)

        @block.scalar
        def _(act):
            give_credits(act, "scalar")
            act.wait_ge(bo_done, 1)
            nc.scalar.activation(bo_all[:], banks[:, WORK, 0:P], ACT.Copy).then_inc(bo_done, 1)
            for g in range(PAIRS):
                act.wait_ge(w_in, 16 * (g + 1))
                if g:
                    act.wait_ge(w_out, 16 * g)
                nc.scalar.activation(wsplit[:, :, 0, :], wload, ACT.Copy).then_inc(w_hi, 1)

            def ffn(t, turn):
                after(act, t.tr, "ln1", turn)
                before(act, t.gu, f"u{HB - 1}", turn)
                nc.scalar.activation(xth[:, 0, :], banks[:, 0, :], ACT.Copy).then_inc(t.xhi.sem, 1)
                for j in range(HB):
                    after(act, t.gu, f"g{j}", turn)
                    before(act, t.hid, f"h{j}", turn)
                    nc.scalar.activation(gated[:, j, :], banks[:, 1 + j, :], ACT.Silu, scale=FS).then_inc(t.silu.sem, 1)

            with act.Fori(0, CHUNKS) as t:
                ffn(pa, t)
                after(act, pa.tr, "ln2", t)
                before(act, pa.m1, "m1", t)
                nc.scalar.activation(x2t, banks[:, 0, :], ACT.Copy).then_inc(pa.xhi.sem, 1)
                after(act, pa.m1, "m1", t)
                nc.scalar.activation(y1, banks[:, 1, :], ACT.Silu, bias=b1_sb[:]).then_inc(pa.y1.sem, 1)
                after(act, pa.m2, "m2", t)
                before(act, pa.hstore, "h", t)
                nc.scalar.activation(hch[:, 0, :], banks[:, 2, :], ACT.Identity, bias=b2_sb[:]).then_inc(pa.hhi.sem, 1)

            def hi(kind, j, n, r):
                name = f"{kind}{j}"
                bank = WORK if name in ("q0", "k0") else ATTN
                dst = qs[r] if kind == "q" else [k[:, 0, :] for k in ks[r]]
                after(act, slots, "b", n)
                after(act, proj, name, n)
                if name in ("q0", "k0"):
                    before(act, kdup, "B", n)
                for h in range(2):
                    last = nc.scalar.activation(dst[h][half(h), j * BANK:(j + 1) * BANK], banks[half(h), bank, :], ACT.Identity,
                                                bias=bslot[half(h), 0:1] if kind == "q" else bslot[half(h), 1:2])
                last.then_inc(hi_done.sem, 1)

            def values(j, n, r):
                after(act, proj, f"v{j}", n)
                nc.scalar.activation(vs[r][:, 4 * j:4 * j + 4, :], banks[:, WORK if j == 0 else ATTN, :].rearrange("p (m d) -> p m d", d=P),
                                     ACT.Copy).then_inc(v_done.sem, 1)

            def exps(u, i):
                c = u[0]
                before(act, pv, f"c{c}", i)
                before(act, dsum if u in DVE_SUMS else psum, unit(u), i)
                for n, (b0, b1) in enumerate(parts(c)):
                    after(act, shifted, f"{unit(u)}.{n}", i)
                    w = min(b1 * BANK, width(c)) - b0 * BANK
                    src = banks[:, RING[u] + b0:RING[u] + b1, :].rearrange("p b n -> p (b n)")
                    nc.scalar.activation(probs[u][:, b0 * BANK:b0 * BANK + w], src[:, 0:w], ACT.Exp, scale=DH ** -0.5).then_inc(exped.sem, 1)

            def pair(i, r, more):
                if more:
                    before(act, scores, "0Bb", i)
                    before(act, pv, "c0", i)
                    hi("q", 0, i + 1, 1 - r)
                    hi("q", 1, i + 1, 1 - r)
                exps((3, 0), i)
                exps((1, 0), i)
                if more:
                    hi("k", 0, i + 1, 1 - r)
                    hi("k", 1, i + 1, 1 - r)
                    values(0, i + 1, 1 - r)
                    values(1, i + 1, 1 - r)
                exps((3, 1), i)
                exps((1, 1), i)
                exps((2, 0), i)
                exps((2, 1), i)
                exps((0, 0), i)
                exps((0, 1), i)

            for kind in "qk":
                for j in range(2):
                    hi(kind, j, 0, 0)
            values(0, 0, 0)
            values(1, 0, 0)
            with act.Fori(0, TURNS // 2 - 1) as i2:
                pair(i2 * 2, 0, True)
                pair(i2 * 2 + 1, 1, True)
            pair(TURNS - 2, 0, True)
            pair(TURNS - 1, 1, False)

            with act.Fori(0, CHUNKS) as t:
                ffn(pd, t)

        @block.vector
        def _(dve):
            give_credits(dve, "vector")
            steps = Steps(dve, dve_step)
            nc.vector.memset(ones64[:], 1.0).then_inc(consts, 1)
            nc.vector.memset(ones_row[:], 1.0).then_inc(consts, 1)
            nc.vector.memset(bvx[:], 1.0).then_inc(consts, 1)
            dve.wait_ge(consts, 3)
            nc.vector.tensor_scalar(minus1[:], bvx[:, 0, :], -1.0, None, ALU.mult).then_inc(consts, 1)
            for u in UNITS:
                nc.vector.tensor_scalar(maxrows[u][:, 0:P], bvx[:, 0, :], 0.0, None, ALU.mult).then_inc(consts, 1)
                nc.vector.tensor_scalar(maxrows[u][:, P:QC], bvx[:, 0, :], 0.0, None, ALU.mult).then_inc(consts, 1)
            dve.wait_ge(consts, 4 + 2 * len(UNITS))
            dve.wait_ge(loaded, 16 * 11)
            for g in range(PAIRS):
                nc.vector.tensor_scalar(bvx[:, g, :], bvx[:, g, :], bv_sb[:, g:g + 1], None, ALU.mult).then_inc(bvx_ready, 1)
            nc.vector.tensor_copy(wff[:], iload[:, 0:2 * HID].rearrange("p (j n) -> p j n", n=P)).then_inc(consts, 1)
            nc.vector.tensor_copy(wdn[:], iload[:, 2 * HID:3 * HID].rearrange("p (j n) -> p j n", n=P)).then_inc(consts, 1)
            for g in range(PAIRS):
                dve.wait_ge(w_hi, g + 1)
                dve.wait_ge(w_in, 16 * (g + 1))
                if g:
                    dve.wait_ge(w_out, 16 * g)
                nc.vector.tensor_tensor(wsplit[:, :, 1, :], wload, wsplit[:, :, 0, :], ALU.subtract).then_inc(w_lo, 1)

            def layernorm(t, ln, src, turn):
                for k in range(CT):
                    nc.vector.bn_stats(stats[:, k, :], src[:, k, :]).then_inc(t.stat.sem, 1)
                after(dve, t.stat, f"{ln}{CT - 1}s", turn)
                dve.sem_inc(idle, 1)
                for k in range(CT):
                    nc.vector.bn_aggr(mv[:, k, :], stats[:, k, :]).then_inc(t.stat.sem, 1)
                (before if ln == "ln1" else after)(dve, t.tr, t.tr.events[-1] if ln == "ln1" else "ln1", turn)
                after(dve, t.rstd, ln, turn)
                for k in range(CT):
                    last = nc.vector.tensor_scalar(xn[:, k, :], src[:, k, :], mv[:, k, 0:1], rstd[:, k:k + 1], ALU.subtract, ALU.mult)
                last.then_inc(t.norm.sem, 1)

            def ffn(t, turn, r):
                after(dve, t.xin, "x", turn)
                layernorm(t, "ln1", xin[r], turn)
                after(dve, t.xhi, "ln1", turn)
                nc.vector.tensor_tensor(xth[:, 1, :], banks[:, 0, :], xth[:, 0, :], ALU.subtract).then_inc(t.xlo.sem, 1)
                for j in range(HB):
                    after(dve, t.silu, f"g{j}", turn)
                    after(dve, t.gu, f"u{j}", turn)
                    before(dve, t.down, "d", turn)
                    nc.vector.tensor_tensor(hidden[:, j, :], gated[:, j, :], banks[:, 1 + HB + j, :], ALU.mult).then_inc(t.hid.sem, 1)
                after(dve, t.down, "d", turn)
                if t.first:
                    before(dve, t.x1b, "x1b", turn)
                else:
                    before(dve, t.store, "s", turn)
                nc.vector.scalar_tensor_tensor(out=x1[:].rearrange("p k d -> p (k d)"), in0=banks[:, WORK, :], scalar=0.5 * FS * FS,
                                               in1=xin[r][:].rearrange("p k d -> p (k d)"), op0=ALU.mult, op1=ALU.add).then_inc(t.x1.sem, 1)

            with dve.Fori(0, CHUNKS // 2) as t2:
                for r in range(2):
                    t = t2 * 2 + r
                    ffn(pa, t, r)
                    after(dve, pa.x1, "x1", t)
                    layernorm(pa, "ln2", x1, t)
                    after(dve, pa.hhi, "h", t)
                    before(dve, pa.hstore, "h", t)
                    nc.vector.scalar_tensor_tensor(out=hch[:, 1, :], in0=banks[:, 2, :], scalar=b2_sb[:], in1=hch[:, 0, :],
                                                   op0=ALU.add, op1=ALU.subtract).then_inc(pa.hlo.sem, 1)

            def lo(kind, j, n, r):
                name = f"{kind}{j}"
                bank = WORK if name in ("q0", "k0") else ATTN
                after(dve, hi_done, name, n)
                for h in range(2):
                    cols = slice(j * BANK, (j + 1) * BANK)
                    high, low = (qs[r][h][half(h), cols], qs[r][h][half(1 - h), cols]) if kind == "q" else \
                                (ks[r][h][half(h), 0, cols], ks[r][h][half(h), 1, cols])
                    last = nc.vector.scalar_tensor_tensor(out=low, in0=banks[half(h), bank, :], in1=high,
                                                          scalar=bslot[half(h), 0:1] if kind == "q" else bslot[half(h), 1:2],
                                                          op0=ALU.add, op1=ALU.subtract)
                last.then_inc(lo_done.sem, 1)

            def block_max(u, i):
                c, acc, b0 = u[0], blockmax[u], RING[u]
                last_bank = banks[:, b0 + c, :]
                before(dve, gmax, unit(u), i)
                if c:
                    after(dve, scores, unit(u) + "a", i)
                    steps.mark(nc.vector.tensor_reduce(acc[:], banks[:, b0:b0 + c, :].rearrange("p b (s q) -> p q b s", s=2), AX.XY, ALU.max))
                after(dve, scores, unit(u) + "b", i)
                if c:
                    steps.wait()
                    steps.mark(nc.vector.tensor_tensor(acc[:], last_bank[:, 0:QC], acc[:], ALU.max))
                else:
                    steps.mark(nc.vector.tensor_copy(acc[:], last_bank[:, 0:QC]))
                partial = pieces(c)[2 * c + 1:]
                for n, (_, col, w, q0) in enumerate(partial):
                    steps.wait()
                    col -= c * BANK
                    m = nc.vector.tensor_tensor(acc[:, q0:q0 + w], last_bank[:, col:col + w], acc[:, q0:q0 + w], ALU.max)
                    if n == len(partial) - 1:
                        m.then_inc(maxed.sem, 1)
                    else:
                        steps.mark(m)

            def max_rows(u, i):
                before(dve, shifted, f"{unit(u)}.{len(parts(u[0])) - 1}", i)
                after(dve, gmax, unit(u), i)
                steps.mark(nc.vector.tensor_copy(maxrows[u][0:1, :], rowmax[u][0:1, :]))
                steps.wait()
                nc.vector.tensor_tensor(maxrows[u][32:33, :], rowmax[u][0:1, :], maxrows[u][0:1, :], ALU.subtract).then_inc(rows.sem, 1)

            def key_sum(u, i):
                c, pr, acc = u[0], probs[u], keysum[u]
                after(dve, exped, f"{unit(u)}.{len(parts(c)) - 1}", i)
                before(dve, pv, f"c{c}", i)
                full = 2 * c + 1
                steps.mark(nc.vector.tensor_reduce(acc[:], pr[:, 0:full * QC].rearrange("p (s q) -> p q s", s=full), AX.X, ALU.add))
                partial = pieces(c)[full:]
                for n, (_, col, w, q0) in enumerate(partial):
                    steps.wait()
                    add = nc.vector.tensor_tensor(acc[:, q0:q0 + w], acc[:, q0:q0 + w], pr[:, col:col + w], ALU.add)
                    if n == len(partial) - 1:
                        add.then_inc(dsum.sem, 1)
                    else:
                        steps.mark(add)

            def normalise(c, i):
                after(dve, pv, f"c{c}", i)
                before(dve, wo_done, "o1", i)
                k = CORDER.index(c)
                if k:
                    after(dve, normed, f"c{CORDER[k - 1]}", i)
                else:
                    before(dve, normed, f"c{CORDER[-1]}", i)
                steps.mark(nc.vector.reciprocal(rsum[:], banks[:, ATTN, QC:2 * QC]))
                steps.wait()
                nc.vector.tensor_tensor(attn[:, c * QC:(c + 1) * QC], banks[:, ATTN, 0:QC], rsum[:], ALU.mult).then_inc(normed.sem, 1)

            def add_output(j, i, at):
                if j == 0:
                    before(dve, wo_added, "o1", i)
                after(dve, wo_done, f"o{j}", i)
                here = xres[:, bass.ds(at + j * BANK, BANK)]
                nc.vector.tensor_tensor(here, banks[:, 2 + j, :], here, ALU.add).then_inc(wo_added.sem, 1)

            def pair(i, r, more):
                steps.begin(i)
                at = dve.snap((i // PAIRS) * N) if not isinstance(i, int) else (i // PAIRS) * N
                block_max((3, 0), i)
                block_max((1, 0), i)
                if more:
                    before(dve, scores, "0Bb", i)
                    lo("q", 0, i + 1, 1 - r)
                max_rows((3, 0), i)
                max_rows((1, 0), i)
                if more:
                    lo("q", 1, i + 1, 1 - r)
                    lo("k", 0, i + 1, 1 - r)
                block_max((3, 1), i)
                block_max((1, 1), i)
                if more:
                    lo("k", 1, i + 1, 1 - r)
                max_rows((3, 1), i)
                max_rows((1, 1), i)
                key_sum((3, 0), i)
                key_sum((3, 1), i)
                block_max((2, 0), i)
                block_max((2, 1), i)
                max_rows((2, 0), i)
                max_rows((2, 1), i)
                normalise(3, i)
                block_max((0, 0), i)
                block_max((0, 1), i)
                max_rows((0, 0), i)
                max_rows((0, 1), i)
                normalise(1, i)
                normalise(2, i)
                normalise(0, i)
                add_output(0, i, at)
                add_output(1, i, at)
                steps.end()

            for kind in "qk":
                for j in range(2):
                    lo(kind, j, 0, 0)
            with dve.Fori(0, TURNS // 2 - 1) as i2:
                pair(i2 * 2, 0, True)
                pair(i2 * 2 + 1, 1, True)
            pair(TURNS - 2, 0, True)
            pair(TURNS - 1, 1, False)

            with dve.Fori(0, CHUNKS // 2) as t2:
                for r in range(2):
                    ffn(pd, t2 * 2 + r, r)

        @block.tensor
        def _(pe):
            give_credits(pe, "tensor")
            mm = nc.tensor.matmul
            pe.wait_ge(loaded, 16 * 11)
            pe.wait_ge(consts, 2)
            pe.wait_ge(bvx_ready, PAIRS)
            for g in range(PAIRS):
                mm(banks[:, WORK, 0:P], bvx[:, g, :], wo_sb[:, g, :], start=(g == 0), stop=False)
            mm(banks[:, WORK, 0:P], ones_row[:], bo_row[:], start=False, stop=True).then_inc(bo_done, 1)
            pe.wait_ge(gp_const, 6)
            pe.wait_ge(consts, 6 + 2 * len(UNITS))

            def transposed(t, ln, turn):
                after(pe, t.norm, ln, turn)
                for k in range(CT):
                    last = nc.tensor.transpose(banks[:, 0, k * P:(k + 1) * P], xn[:, k, :], ident[:])
                last.then_inc(t.tr.sem, 1)

            def ffn(t, turn):
                if t.first:
                    before(pe, t.xhi, "ln2", turn)
                else:
                    before(pe, t.xlo, "ln1", turn)
                transposed(t, "ln1", turn)
                after(pe, t.xlo, "ln1", turn)
                if t.first:
                    before(pe, t.hlo, "h", turn)
                for j in range(2 * HB):
                    if j < HB:
                        before(pe, t.silu, f"g{j}", turn)
                    else:
                        before(pe, t.hid, f"h{j - HB}", turn)
                    mm(banks[:, 1 + j, :], wff[:, j, :], xth[:, 0, :], start=True, stop=False)
                    mm(banks[:, 1 + j, :], wff[:, j, :], xth[:, 1, :], start=False, stop=True).then_inc(t.gu.sem, 1)
                before(pe, t.x1, "x1", turn)
                after(pe, t.hid, f"h{HB - 1}", turn)
                for k in range(CT):
                    for j in range(HB):
                        last = mm(banks[:, WORK, k * P:(k + 1) * P], hidden[:, j, k * P:(k + 1) * P], wdn[:, j, :],
                                  start=(j == 0), stop=(j == HB - 1))
                last.then_inc(t.down.sem, 1)

            with pe.Fori(0, CHUNKS) as t:
                ffn(pa, t)
                transposed(pa, "ln2", t)
                after(pe, pa.xhi, "ln2", t)
                mm(banks[:, 1, :], w1_sb[:], x2t, start=True, stop=True).then_inc(pa.m1.sem, 1)
                after(pe, pa.y1, "y1", t)
                mm(banks[:, 2, :], w2_sb[:], y1, start=True, stop=True).then_inc(pa.m2.sem, 1)

            def project(kind, j, n):
                name = f"{kind}{j}"
                bank = banks[:, WORK if name in ("q0", "k0", "v0") else ATTN, :]
                w = wslot[:, "qkv".index(kind)]
                if name == "q0":
                    after(pe, slots, "b", n)
                    before(pe, v_done, "v0", n)
                elif name == "q1":
                    before(pe, v_done, "v1", n)
                    pe.wait_ge(normed.sem, normed.per_pass * n if not isinstance(n, int) else normed.per_pass)
                else:
                    after(pe, lo_done, {"k0": "q0", "k1": "q1", "v0": "k0", "v1": "k1"}[name], n)
                if kind != "v":
                    toks = slice(j * BANK, (j + 1) * BANK)
                    mm(bank, w[:, 0, :], hb[:, 0, toks], start=True, stop=False)
                    mm(bank, w[:, 0, :], hb[:, 1, toks], start=False, stop=False)
                    last = mm(bank, w[:, 1, :], hb[:, 0, toks], start=False, stop=True)
                else:
                    for m in range(4):
                        toks = slice((4 * j + m) * P, (4 * j + m + 1) * P)
                        dst = bank[:, m * P:(m + 1) * P]
                        mm(dst, hb[:, 0, toks], w[:, 0, :], start=True, stop=False)
                        mm(dst, hb[:, 0, toks], w[:, 1, :], start=False, stop=False)
                        last = mm(dst, hb[:, 1, toks], w[:, 0, :], start=False, stop=True)
                last.then_inc(proj.sem, 1)

            def freed(u, b, i):
                bank = RING[u] + b
                k = UNITS.index(u)
                for v in UNITS[k - 1::-1] if k else []:
                    if RING[v] <= bank <= RING[v] + v[0]:
                        n = (bank - RING[v]) // 2
                        return after(pe, exped, f"{unit(v)}.{n}", i)
                if bank in (2, 3):
                    return before(pe, wo_added, f"o{bank - 2}", i)
                for v in UNITS[::-1]:
                    if RING[v] <= bank <= RING[v] + v[0]:
                        return before(pe, exped, f"{unit(v)}.{(bank - RING[v]) // 2}", i)

            def score(u, i, r):
                c, h = u
                if u == UNITS[0]:
                    after(pe, kdup, "B", i)
                for kb, col, w, q0 in pieces(c):
                    b = col // BANK
                    first = col % BANK == 0
                    if first:
                        if b == c and c:
                            last.then_inc(scores.sem, 1)
                        freed(u, b, i)
                    dst = banks[:, RING[u] + b, col % BANK:col % BANK + w]
                    qcols = slice(c * QC + q0, c * QC + q0 + w)
                    m0 = c * QC + q0 - (kb * P - WINDOW)
                    edge = min(P - m0, w) if m0 < P else 0
                    mm(dst, ks[r][h][:, 0, kb * P:(kb + 1) * P], qs[r][h][:, qcols], start=first, stop=False, skip_group_check=True)
                    last = mm(dst, ks[r][h][:, 1, kb * P:(kb + 1) * P], qs[r][h][:, qcols], start=False, stop=not edge, skip_group_check=True)
                    if edge:
                        last = mm(dst[:, 0:edge], ident16[:], mask16[:, m0:m0 + edge], start=False, stop=True, skip_group_check=True)
                last.then_inc(scores.sem, 1)

            def shift(u, i):
                c = u[0]
                after(pe, rows, unit(u), i)
                for b0, b1 in parts(c):
                    for b in range(b0, b1):
                        bank = banks[:, RING[u] + b, :]
                        here = [(col - b * BANK, w, q0) for _, col, w, q0 in pieces(c) if col // BANK == b]
                        if len(here) == 2 and here[1][1] == QC:
                            last = mm(bank.rearrange("p (s q) -> p s q", s=2), minus1[:], maxrows[u][:].unsqueeze(1).to_broadcast([P, 2, QC]),
                                      start=False, stop=True, skip_group_check=True)
                        else:
                            for col, w, q0 in here:
                                last = mm(bank[:, col:col + w], minus1[:], maxrows[u][:, q0:q0 + w], start=False, stop=True, skip_group_check=True)
                    last.then_inc(shifted.sem, 1)

            def attend(c, i, r):
                k = CORDER.index(c)
                if k == 0:
                    after(pe, v_done, "v1", i)
                else:
                    after(pe, normed, f"c{CORDER[k - 1]}", i)
                after(pe, exped, f"{c}B.{len(parts(c)) - 1}", i)
                ps = pieces(c)
                for kb, col, w, q0 in ps:
                    for h in range(2):
                        mm(banks[half(h), ATTN, q0:q0 + w], vs[r][:, kb, half(h)], probs[c, h][:, col:col + w],
                           start=(kb == 0), stop=(kb == ps[-1][0]), skip_group_check=True)
                for h in range(2):
                    after(pe, dsum if (c, h) in DVE_SUMS else psum, unit((c, h)), i)
                    last = mm(banks[half(h), ATTN, QC:2 * QC], ones64[:], keysum[c, h][:], start=True, stop=True, skip_group_check=True)
                last.then_inc(pv.sem, 1)

            def output(j, i, g):
                after(pe, normed, "c0", i)
                after(pe, exped, "2A.1" if j == 0 else "2B.0", i)
                for m in range(4):
                    tile = slice((4 * j + m) * P, (4 * j + m + 1) * P)
                    last = mm(banks[:, 2 + j, m * P:(m + 1) * P], attn[:, tile], wo_sb[:, bass.ds(g, 1), :].rearrange("p g n -> p (g n)"),
                              start=True, stop=True)
                last.then_inc(wo_done.sem, 1)

            def pair(i, r, more):
                g = pe.snap(i % PAIRS) if not isinstance(i, int) else i % PAIRS
                score((3, 0), i, r)
                score((1, 0), i, r)
                if more:
                    project("q", 0, i + 1)
                    project("q", 1, i + 1)
                    project("k", 0, i + 1)
                shift((3, 0), i)
                shift((1, 0), i)
                score((3, 1), i, r)
                score((1, 1), i, r)
                if more:
                    project("k", 1, i + 1)
                    project("v", 0, i + 1)
                    project("v", 1, i + 1)
                shift((3, 1), i)
                shift((1, 1), i)
                score((2, 0), i, r)
                score((2, 1), i, r)
                attend(3, i, r)
                shift((2, 0), i)
                shift((2, 1), i)
                score((0, 0), i, r)
                score((0, 1), i, r)
                attend(1, i, r)
                shift((0, 0), i)
                shift((0, 1), i)
                attend(2, i, r)
                attend(0, i, r)
                output(0, i, g)
                output(1, i, g)

            after(pe, pa.hlo, "h", CHUNKS - 1)
            after(pe, pa.x1, "x1", CHUNKS - 1)
            for kind in "qkv":
                for j in range(2):
                    project(kind, j, 0)
            with pe.Fori(0, TURNS // 2 - 1) as i2:
                pair(i2 * 2, 0, True)
                pair(i2 * 2 + 1, 1, True)
            pair(TURNS - 2, 0, True)
            pair(TURNS - 1, 1, False)

            after(pe, wo_added, "o1", TURNS - 1)
            with pe.Fori(0, CHUNKS) as t:
                ffn(pd, t)


def kernel(L0_attn_x, L0_attn_W1, L0_attn_b1, L0_attn_W2, L0_attn_b2, L0_attn_Wg, L0_attn_bg, L0_attn_Wo, L0_attn_bo,
           L0_ffn_w_gate, L0_ffn_w_up, L0_ffn_w_down):
    import numpy as np
    import concourse.bacc as bacc
    from concourse.bass_utils import run_bass_kernel_spmd

    x = np.asarray(L0_attn_x)
    bg = np.asarray(L0_attn_bg).reshape(3, -1, P)
    arrays = {
        "x": x.reshape(-1, x.shape[-1]),
        "w1t": np.asarray(L0_attn_W1).T, "b1": np.asarray(L0_attn_b1).reshape(-1, 1),
        "w2t": np.asarray(L0_attn_W2).T, "b2": np.asarray(L0_attn_b2).reshape(-1, 1),
        "wqkvt": np.asarray(L0_attn_Wg).T,
        "bqk": bg[0:2].transpose(2, 1, 0).reshape(P, -1), "bv": bg[2].T,
        "wot": np.asarray(L0_attn_Wo).T, "bo": np.asarray(L0_attn_bo).reshape(1, -1),
        "wgatet": np.asarray(L0_ffn_w_gate).T, "wupt": np.asarray(L0_ffn_w_up).T, "wdownt": np.asarray(L0_ffn_w_down).T,
    }
    nc = bacc.Bacc("TRN2", target_bir_lowering=False, num_devices=1)
    feed, args = {}, []
    for name, a in arrays.items():
        feed[f"in_{name}"] = np.ascontiguousarray(a)
        args.append(nc.dram_tensor(f"in_{name}", a.shape, mybir.dt.from_np(a.dtype), kind="ExternalInput").ap())
    out = nc.dram_tensor("y", arrays["x"].shape, F32, kind="ExternalOutput").ap()
    macaron(nc, *args, out)
    r = run_bass_kernel_spmd(nc, [feed], core_ids=[0])
    return r.results[0]["y"].reshape(x.shape)
```

```python
from contextlib import ExitStack

import concourse.bass as bass
from concourse import mybir

F32 = mybir.dt.float32
F32R = mybir.dt.float32r
BF16 = mybir.dt.bfloat16
I32 = mybir.dt.int32
ALU = mybir.AluOpType
ACT = mybir.ActivationFunctionType
AX = mybir.AxisListType
MAX = bass.bass_isa.ReduceOp.max

P = 128
BANK = 512
MASKED = -3.0e38
EPS = 1e-5


class Tally:

    def __init__(self, sem, events, step=1):
        self.sem, self.events, self.step = sem, list(events), step
        self.per_pass = len(self.events) * step

    def after(self, event, turn):
        return (turn + 1) * self.per_pass + (self.events.index(event) + 1) * self.step

    def before(self, event, turn):
        return turn * self.per_pass + (self.events.index(event) + 1) * self.step


def macaron(nc, x, w1t, b1, w2t, b2, wqkvt, bqk, bv, wot, bo, wgatet, wupt, wdownt, out):
    TOK, D = x.shape
    BATCH, N = 4, TOK // 4
    DH, WINDOW = 64, 64
    PAIRS = wot.shape[0] // P
    TURNS = BATCH * PAIRS
    HID = wgatet.shape[1]
    HB = HID // P
    FS = 1.0 / 127.0
    CH = 512
    CHUNKS = TOK // CH
    CT = CH // P
    QC = 256
    assert D == P and N == 1024 and CH == BANK

    UNITS = [(3, 0), (1, 0), (3, 1), (1, 1), (2, 0), (2, 1), (0, 0), (0, 1)]
    RING = {(3, 0): 0, (1, 0): 4, (3, 1): 0, (1, 1): 4, (2, 0): 0, (2, 1): 3, (0, 0): 0, (0, 1): 1}
    SHARED = 4
    T_BANK = {"ln1": 0, "ln2": 7}
    WORK, ATTN = 7, 6
    PROJ = {"k0": WORK, "k1": WORK, "q0": ATTN, "q1": WORK, "v0": 4, "v1": 5}

    def pieces(c):
        full = [(kb, kb * QC, QC, 0) for kb in range(2 * c + 1)]
        part = [(2 * c + 1, (2 * c + 1) * QC, QC - WINDOW, WINDOW)]
        last = [(2 * c + 2, (2 * c + 2) * QC - WINDOW, WINDOW, QC - WINDOW)] if 2 * c + 2 < N // P else []
        return full + part + last

    def width(c):
        return sum(w for _, _, w, _ in pieces(c))

    def parts(c):
        return [(b, min(b + 2, c + 1)) for b in range(0, c + 1, 2)]

    def unit(u):
        return f"{u[0]}{'AB'[u[1]]}"

    with ExitStack() as ctx:
        def sb(name, shape, dt=F32):
            return ctx.enter_context(nc.sbuf_tensor(name, shape, dt))

        def sem(name):
            return ctx.enter_context(nc.semaphore(name))

        ident = sb("ident", [P, P])
        ident16 = sb("ident16", [P, P], BF16)
        mask16 = sb("mask16", [P, P], BF16)
        ones64 = sb("ones64", [P, DH])
        minus1 = sb("minus1", [P, P], F32R)
        w1_sb = sb("w1_sb", [P, P])
        w2_sb = sb("w2_sb", [P, P])
        b1_sb = sb("b1_sb", [P, 1])
        b2_sb = sb("b2_sb", [P, 1])
        bqk_sb = sb("bqk_sb", [P, PAIRS, 2])
        bv_sb = sb("bv_sb", [P, PAIRS])
        bo_row = sb("bo_row", [1, P])
        ones_row = sb("ones_row", [1, P])
        bo_all = sb("bo_all", [P, P])
        wo_sb = sb("wo_sb", [P, PAIRS, P])
        wff = sb("wff", [P, 2 * HB, P], F32R)
        wdn = sb("wdn", [P, HB, P])
        xres = sb("xres", [P, TOK // P * D])
        probs = {(c, h): sb(f"probs{c}{h}", [P, (c + 1) * BANK]) for c in range(4) for h in range(2)}
        blockmax_of = [sb(f"blockmax{k}", [P, QC]) for k in range(SHARED)]
        rowmax_of = [sb(f"rowmax{k}", [P, QC]) for k in range(SHARED)]
        blockmax = {u: blockmax_of[k % SHARED] for k, u in enumerate(UNITS)}
        rowmax = {u: rowmax_of[k % SHARED] for k, u in enumerate(UNITS)}
        maxrows = {u: sb(f"maxrows{unit(u)}", [P, QC], F32R) for u in UNITS}
        keysum = {u: sb(f"keysum{unit(u)}", [P, QC]) for u in UNITS}
        qs = [[sb(f"qs{r}{h}", [P, N], F32R) for h in range(2)] for r in range(2)]
        ks = [[sb(f"ks{r}{h}", [P, 2, N], F32R) for h in range(2)] for r in range(2)]
        vs = [sb(f"vs{r}", [P, N // P, P]) for r in range(2)]
        kt = sb("kt", [P, 2, N], F32R)
        qt = sb("qt", [P, 2, N], F32R)
        osum = [sb(f"osum{r}", [P, BANK]) for r in range(2)]
        attn = [sb(f"attn{r}", [P, N]) for r in range(2)]
        rsum = sb("rsum", [P, QC])
        hb = [sb(f"hb{r}", [P, 2, N], F32R) for r in range(2)]
        wslot = [sb(f"wslot{r}", [P, 3, 2, P], F32R) for r in range(2)]
        bslot = [sb(f"bslot{r}", [P, 2]) for r in range(2)]
        def tokens(buf, k):
            return buf[:, k * CH:(k + 1) * CH].rearrange("p (k d) -> p k d", d=D)

        LNS = ["ln1", "ln2"]
        xn = {ln: tokens(attn[1], k) for k, ln in enumerate(LNS)}
        stats = {ln: sb(f"stats_{ln}", [P, CT, 6]) for ln in LNS}
        mv = {ln: sb(f"mv_{ln}", [P, CT, 2]) for ln in LNS}
        rstd = {ln: sb(f"rstd_{ln}", [P, CT]) for ln in LNS}
        veps = {ln: sb(f"veps_{ln}", [P, CT]) for ln in LNS}
        mhalf = sb("mhalf", [P, CT])
        xth = qs[0][0][:].rearrange("p (s n) -> p s n", s=2)
        hch = qs[0][1][:].rearrange("p (s n) -> p s n", s=2)
        gated = probs[3, 0][:, 0:HB * CH].rearrange("p (j n) -> p j n", j=HB)
        hidden = probs[3, 1][:, 0:HB * CH].rearrange("p (j n) -> p j n", j=HB)
        x2t = probs[2, 0][:, 0:CH]
        y1 = probs[2, 0][:, CH:2 * CH]
        iload = probs[3, 1][:, 0:3 * HID].bitcast(I32)
        bvx = attn[0][:].rearrange("p (g n) -> p g n", n=P)
        WPARTS, WCOLS = PAIRS // 2, 2 * 3 * P
        wload = [b.rearrange("p (g t n) -> p g t n", g=2, t=3) for b in
                 (probs[2, 1][:, 0:WCOLS], probs[2, 1][:, WCOLS:2 * WCOLS], probs[1, 0][:, 0:WCOLS], probs[1, 1][:, 0:WCOLS])]
        wsplit = [ks[k // 2][k % 2][:].rearrange("p s n -> p (s n)")[:, 0:2 * WCOLS].rearrange("p (g t s n) -> p g t s n", g=2, t=3, s=2)
                  for k in range(WPARTS)]

        banks = ctx.enter_context(nc.psum_tensor("banks", [P, 8, BANK], F32))

        h_dram = nc.dram_tensor("h_scratch", [2, P, TOK], F32, kind="Internal").ap()
        w_dram = nc.dram_tensor("w_scratch", [P, PAIRS, 3 * 2 * P], F32, kind="Internal").ap()

        ints_loaded = sem("ints_loaded")
        x_loaded = sem("x_loaded")
        loaded = sem("loaded")
        wq_loaded = sem("wq_loaded")
        consts = sem("consts")
        weights_ready = sem("weights_ready")
        gp_const = sem("gp_const")
        bvx_ready = sem("bvx_ready")
        bo_done = sem("bo_done")
        w_hi = sem("w_hi")
        w_lo = sem("w_lo")
        w_stored = sem("w_stored")
        stored = sem("stored")
        idle = sem("idle")

        class Phase:
            pass

        def phase(name, lns):
            t = Phase()
            T = lambda n, ev, step=1: Tally(sem(f"{name}_{n}"), ev, step)
            t.stat = {ln: T(f"stat_{ln}", [f"{s}{k}" for s in "sa" for k in range(CT)]) for ln in lns}
            t.rstd = {ln: T(f"rstd_{ln}", ["e", "r"]) for ln in lns}
            t.norm = {ln: T(f"norm_{ln}", ["n"]) for ln in lns}
            t.tr = {ln: T(f"tr_{ln}", ["t"]) for ln in lns}
            t.copied = {ln: T(f"copied_{ln}", ["c"]) for ln in lns}
            t.xlo = T("xlo", ["l"])
            t.gu = T("gu", [f"g{j}" for j in range(HB)] + [f"u{j}" for j in range(HB)])
            t.silu = T("silu", [f"g{j}" for j in range(HB)])
            t.hid = T("hid", [f"h{j}" for j in range(HB)])
            t.down = T("down", ["d"])
            t.x1 = T("x1", ["x"])
            t.biased = T("biased", ["b"])
            t.m1 = T("m1", ["m"])
            t.y1 = T("y1", ["y"])
            t.m2 = T("m2", ["m"])
            t.hhi = T("hhi", ["h"])
            t.hlo = T("hlo", ["h"])
            t.hstore = T("hstore", ["h"], 16)
            return t

        pa, pd = phase("a", LNS), phase("d", LNS[:1])

        T = lambda n, ev, step=1: Tally(sem(n), ev, step)
        HALVES = ["k0", "k1", "q0", "q1"]
        score_events = [e for u in UNITS for e in ([unit(u) + "a"] if u[0] else []) + [unit(u) + "b"]]
        piece_events = [f"{unit(u)}.{n}" for u in UNITS for n in range(len(parts(u[0])))]
        scores = T("scores", score_events)
        maxed = T("maxed", [unit(u) for u in UNITS])
        gmax = T("gmax", [unit(u) for u in UNITS])
        rows = T("rows", [unit(u) for u in UNITS])
        shifted = T("shifted", piece_events)
        exped = T("exped", piece_events)
        DVE_SUMS = [(3, 0), (3, 1)]
        POOL_SUMS = [(1, 0), (1, 1), (2, 0), (2, 1), (0, 0), (0, 1)]
        dsum = T("dsum", [unit(u) for u in DVE_SUMS])
        psum = T("psum_", [unit(u) for u in POOL_SUMS])
        CORDER = [3, 1, 2, 0]
        pv = T("pv", [f"c{c}" for c in CORDER])
        evac = T("evac", [f"c{c}" for c in CORDER])
        normed = T("normed", [f"c{c}" for c in CORDER])
        proj = T("proj", HALVES + ["v0", "v1"])
        hi_done = T("hi_done", HALVES)
        lo_done = T("lo_done", HALVES)
        v_done = T("v_done", ["v0", "v1"])
        stacks = T("stacks", [f"{t}{h}{s}" for t in "kq" for h in "AB" for s in "01"], 16)
        slots = T("slots", ["h", "w", "b"], 16)
        wo_done = T("wo_done", ["o0", "o1"])
        wo_added = T("wo_added", ["o0", "o1"])
        dve_step = T("dve_step", range(34))
        pool_step = T("pool_step", range(20))

        credits = {
            "sync": [stacks, slots], "vector": [maxed, rows, dsum, normed, lo_done, wo_added, dve_step],
            "scalar": [exped, hi_done, v_done, evac], "tensor": [scores, shifted, pv, proj, wo_done],
            "gpsimd": [gmax, psum, pool_step],
        }
        for t in (pa, pd):
            credits["sync"] += [t.hstore]
            credits["vector"] += [*t.stat.values(), *t.norm.values(), t.xlo, t.hid, t.x1, t.hlo]
            credits["gpsimd"] += [*t.rstd.values(), t.biased]
            credits["tensor"] += [*t.tr.values(), t.gu, t.down, t.m1, t.m2]
            credits["scalar"] += [*t.copied.values(), t.silu, t.y1, t.hhi]

        def give_credits(eng, name):
            for t in credits[name]:
                eng.sem_inc(t.sem, t.per_pass)

        def after(eng, tally, event, turn):
            eng.wait_ge(tally.sem, tally.after(event, turn))

        def before(eng, tally, event, turn):
            eng.wait_ge(tally.sem, tally.before(event, turn))

        def used_by(eng, tally, u, i):
            k = UNITS.index(u)
            (after if k >= SHARED else before)(eng, tally, unit(UNITS[k - SHARED]), i)

        class Steps:

            def __init__(self, eng, tally):
                self.eng, self.tally = eng, tally

            def begin(self, turn):
                self.turn, self.n = turn, 0

            def mark(self, instruction):
                self.n += 1
                instruction.then_inc(self.tally.sem, 1)

            def wait(self):
                after(self.eng, self.tally, self.n - 1, self.turn)

            def end(self):
                left = len(self.tally.events) - self.n
                assert left >= 0, self.n
                if left:
                    self.eng.sem_inc(self.tally.sem, left)

        def half(h):
            return slice(DH * h, DH * h + DH)

        block = ctx.enter_context(nc.Block())

        @block.sync
        def _(sp):
            give_credits(sp, "sync")
            for dst, src in ((iload[:, 0:HID], wgatet), (iload[:, HID:2 * HID], wupt),
                             (iload[:, 2 * HID:3 * HID].rearrange("p (j n) -> p j n", j=HB), wdownt.rearrange("(j p) n -> p j n", p=P))):
                sp.dma_start(dst, src).then_inc(ints_loaded, 16)
            x_src = x.rearrange("(k p) d -> p k d", p=P)
            resident = xres[:].rearrange("p (k d) -> p k d", d=D)
            half_tiles = TOK // P // 2
            for k in range(2):
                tiles = slice(k * half_tiles, (k + 1) * half_tiles)
                sp.dma_start(resident[:, tiles, :], x_src[:, tiles, :]).then_inc(x_loaded, 16)
            for dst, src in (
                (w1_sb[:], w1t), (w2_sb[:], w2t), (b1_sb[:], b1), (b2_sb[:], b2),
                (bqk_sb[:], bqk.rearrange("p (g t) -> p g t", t=2)), (bv_sb[:], bv),
                (wo_sb[:], wot.rearrange("(g p) n -> p g n", p=P)), (bo_row[:], bo),
            ):
                sp.dma_start(dst, src).then_inc(loaded, 16)
            sp.wait_ge(weights_ready, 2)
            wq_src = wqkvt.rearrange("p (t k g n) -> p k g t n", t=3, k=WPARTS, n=P)
            for k in range(WPARTS):
                for g in range(2):
                    sp.dma_start(wload[k][:, g], wq_src[:, k, g]).then_inc(wq_loaded, 16)
            for k in range(WPARTS):
                sp.wait_ge(w_hi, k + 1)
                sp.wait_ge(w_lo, k + 1)
                sp.dma_start(w_dram[:, 2 * k:2 * k + 2, :].rearrange("p g n -> p (g n)"),
                             wsplit[k].rearrange("p g t s n -> p (g t s n)").bitcast(F32)).then_inc(w_stored, 16)
            with sp.Fori(0, CHUNKS) as t:
                at = sp.snap(t * CH)
                after(sp, pa.hhi, "h", t)
                after(sp, pa.hlo, "h", t)
                sp.dma_start(h_dram[:, :, bass.ds(at, CH)].rearrange("s p n -> p s n"), hch.bitcast(F32)).then_inc(pa.hstore.sem, 16)
            after(sp, pa.hstore, "h", CHUNKS - 1)
            sp.wait_ge(w_stored, 16 * WPARTS)

            def load_slots(n, r):
                h_at = sp.snap((n // PAIRS) * N) if not isinstance(n, int) else 0
                g_at = sp.snap(n % PAIRS) if not isinstance(n, int) else n
                if not (isinstance(n, int) and n == 0):
                    after(sp, slots, "b", n - 1)
                if not isinstance(n, int):
                    after(sp, proj, "v1", n - 2)
                    after(sp, lo_done, "q1", n - 2)
                sp.dma_start(hb[r][:].bitcast(F32), h_dram[:, :, bass.ds(h_at, N)].rearrange("s p n -> p s n")).then_inc(slots.sem, 16)
                sp.dma_start(wslot[r][:].bitcast(F32).rearrange("p t s n -> p (t s n)").unsqueeze(1), w_dram[:, bass.ds(g_at, 1), :]).then_inc(slots.sem, 16)
                sp.dma_start(bslot[r][:].unsqueeze(1), bqk_sb[:, bass.ds(g_at, 1), :]).then_inc(slots.sem, 16)

            def stack(n, r):
                after(sp, hi_done, "k1", n)
                after(sp, lo_done, "k1", n)
                for h in range(2):
                    for s in range(2):
                        sp.dma_start(ks[r][h][half(s)].bitcast(F32), kt[half(h)].bitcast(F32)).then_inc(stacks.sem, 16)
                after(sp, hi_done, "q1", n)
                after(sp, lo_done, "q1", n)
                for h in range(2):
                    for s in range(2):
                        sp.dma_start(qs[r][h][half(s)].bitcast(F32), qt[half(h), s, :].bitcast(F32)).then_inc(stacks.sem, 16)

            load_slots(0, 0)
            load_slots(1, 1)
            stack(0, 0)
            with sp.Fori(0, TURNS // 2 - 1) as i:
                load_slots(i * 2 + 2, 0)
                stack(i * 2 + 1, 1)
                load_slots(i * 2 + 3, 1)
                stack(i * 2 + 2, 0)
            stack(TURNS - 1, 1)

            out_dst = out.rearrange("(k p) d -> p k d", p=P)
            with sp.Fori(0, CHUNKS) as t:
                at = sp.snap(t * CT)
                after(sp, pd.x1, "x", t)
                sp.dma_start(out_dst[:, bass.ds(at, CT), :], resident[:, bass.ds(at, CT), :]).then_inc(stored, 16)
            sp.wait_ge(stored, 16 * CHUNKS)

        @block.gpsimd
        def _(pool):
            give_credits(pool, "gpsimd")
            steps = Steps(pool, pool_step)
            nc.gpsimd.memset(ident[:], 0.0).then_inc(gp_const, 1)
            nc.gpsimd.memset(mask16[:], 0.0).then_inc(gp_const, 1)
            nc.gpsimd.memset(mhalf[:], -0.5).then_inc(gp_const, 1)
            pool.wait_ge(gp_const, 3)
            nc.gpsimd.affine_select(out=ident[:], in_=ident[:], compare_op=ALU.not_equal, fill=1.0, base=0,
                                    pattern=[[-1, P]], channel_multiplier=1).then_inc(gp_const, 1)
            nc.gpsimd.affine_select(out=mask16[:], in_=mask16[:], compare_op=ALU.is_ge, fill=MASKED, base=-1,
                                    pattern=[[1, P]], channel_multiplier=-1).then_inc(gp_const, 1)
            pool.wait_ge(gp_const, 5)
            nc.gpsimd.tensor_copy(ident16[:], ident[:]).then_inc(gp_const, 1)
            pool.wait_ge(gp_const, 6)

            def rstd_of(t, ln, turn):
                after(pool, t.stat[ln], f"a{CT - 1}", turn)
                pool.sem_inc(idle, 1)
                nc.gpsimd.tensor_scalar(veps[ln][:], mv[ln][:, :, 1], EPS, None, ALU.add).then_inc(t.rstd[ln].sem, 1)
                after(pool, t.rstd[ln], "e", turn)
                nc.gpsimd.tensor_tensor(rstd[ln][:], veps[ln][:], mhalf[:], ALU.pow).then_inc(t.rstd[ln].sem, 1)

            def add_bias(turn, at):
                after(pool, pa.norm["ln2"], "n", turn)
                here = xres[:, bass.ds(at, CT * D)].rearrange("p (k d) -> p k d", d=D)
                nc.gpsimd.tensor_tensor(here, here, bo_all[:].unsqueeze(1).to_broadcast([P, CT, P]), ALU.add).then_inc(pa.biased.sem, 1)

            rstd_of(pa, "ln1", 0)
            rstd_of(pa, "ln1", 1)
            pool.wait_ge(bo_done, 2)
            with pool.Fori(1, CHUNKS - 1) as t:
                at = pool.snap((t - 1) * CH)
                rstd_of(pa, "ln2", t - 1)
                rstd_of(pa, "ln1", t + 1)
                add_bias(t - 1, at)
            for t in range(CHUNKS - 2, CHUNKS):
                rstd_of(pa, "ln2", t)
                add_bias(t, t * CH)

            def row_max(u, i):
                used_by(pool, rows, u, i)
                after(pool, maxed, unit(u), i)
                pool.sem_inc(idle, 1)
                nc.gpsimd.partition_all_reduce(rowmax[u][:], blockmax[u][:], P, MAX).then_inc(gmax.sem, 1)

            def key_sum(u, i):
                c, pr, acc = u[0], probs[u], keysum[u]
                after(pool, exped, f"{unit(u)}.{len(parts(c)) - 1}", i)
                before(pool, pv, f"c{c}", i)
                if c == 0:
                    pool.sem_inc(idle, 1)
                    steps.mark(nc.gpsimd.tensor_copy(acc[:, 0:WINDOW], pr[:, 0:WINDOW]))
                rest = pieces(c)[1:]
                for n, (_, col, w, q0) in enumerate(rest):
                    if n:
                        steps.wait()
                    src = acc if n else pr
                    add = nc.gpsimd.tensor_tensor(acc[:, q0:q0 + w], src[:, q0:q0 + w], pr[:, col:col + w], ALU.add)
                    if n == len(rest) - 1:
                        add.then_inc(psum.sem, 1)
                    else:
                        steps.mark(add)

            def pair(i, carry=True):
                steps.begin(i)
                row_max((3, 0), i)
                row_max((1, 0), i)
                if carry:
                    key_sum((0, 0), i - 1)
                    key_sum((0, 1), i - 1)
                row_max((3, 1), i)
                row_max((1, 1), i)
                key_sum((1, 0), i)
                key_sum((1, 1), i)
                row_max((2, 0), i)
                row_max((2, 1), i)
                row_max((0, 0), i)
                row_max((0, 1), i)
                key_sum((2, 0), i)
                key_sum((2, 1), i)
                steps.end()

            pair(0, carry=False)
            with pool.Fori(1, TURNS) as i:
                pair(i)
            steps.begin(TURNS)
            key_sum((0, 0), TURNS - 1)
            key_sum((0, 1), TURNS - 1)

            with pool.Fori(0, CHUNKS) as t:
                rstd_of(pd, "ln1", t)

        @block.scalar
        def _(act):
            give_credits(act, "scalar")

            def copy_transposed(t, ln, turn):
                after(act, t.tr[ln], "t", turn)
                if ln == "ln1":
                    before(act, t.gu, f"u{HB - 1}", turn)
                    nc.scalar.activation(xth[:, 0, :], banks[:, T_BANK[ln], :], ACT.Copy).then_inc(t.copied[ln].sem, 1)
                else:
                    before(act, t.m1, "m", turn)
                    nc.scalar.activation(x2t, banks[:, T_BANK[ln], :], ACT.Copy).then_inc(t.copied[ln].sem, 1)

            def silus(t, turn):
                for j in range(HB):
                    after(act, t.gu, f"g{j}", turn)
                    before(act, t.hid, f"h{j}", turn)
                    nc.scalar.activation(gated[:, j, :], banks[:, 1 + j, :], ACT.Silu, scale=FS).then_inc(t.silu.sem, 1)

            def mlp(turn):
                after(act, pa.m1, "m", turn)
                nc.scalar.activation(y1, banks[:, T_BANK["ln2"], :], ACT.Silu, bias=b1_sb[:]).then_inc(pa.y1.sem, 1)
                after(act, pa.m2, "m", turn)
                before(act, pa.hstore, "h", turn)
                nc.scalar.activation(hch[:, 0, :], banks[:, T_BANK["ln2"], :], ACT.Identity, bias=b2_sb[:]).then_inc(pa.hhi.sem, 1)

            copy_transposed(pa, "ln1", 0)
            silus(pa, 0)
            copy_transposed(pa, "ln1", 1)
            act.wait_ge(bo_done, 1)
            nc.scalar.activation(bo_all[:], banks[:, WORK, 0:P], ACT.Copy).then_inc(bo_done, 1)
            for k in range(WPARTS):
                act.wait_ge(wq_loaded, 16 * 2 * WPARTS)
                nc.scalar.activation(wsplit[k][:, :, :, 0, :], wload[k], ACT.Copy).then_inc(w_hi, 1)
            with act.Fori(1, CHUNKS - 1) as t:
                silus(pa, t)
                copy_transposed(pa, "ln2", t - 1)
                copy_transposed(pa, "ln1", t + 1)
                mlp(t - 1)
            silus(pa, CHUNKS - 1)
            for t in range(CHUNKS - 2, CHUNKS):
                copy_transposed(pa, "ln2", t)
                mlp(t)

            def hi(kind, j, n, r):
                name, dst = f"{kind}{j}", qt if kind == "q" else kt
                before(act, stacks, "qB1", n)
                after(act, proj, name, n)
                nc.scalar.activation(dst[:, 0, j * BANK:(j + 1) * BANK], banks[:, PROJ[name], :], ACT.Identity,
                                     bias=bslot[r][:, 0:1] if kind == "q" else bslot[r][:, 1:2]).then_inc(hi_done.sem, 1)

            def values(j, n, r):
                after(act, proj, f"v{j}", n)
                nc.scalar.activation(vs[r][:, 4 * j:4 * j + 4, :], banks[:, PROJ[f"v{j}"], :].rearrange("p (m d) -> p m d", d=P),
                                     ACT.Copy).then_inc(v_done.sem, 1)

            def evacuate(c, i):
                k = CORDER.index(c)
                after(act, pv, f"c{c}", i)
                (after if k >= 2 else before)(act, normed, f"c{CORDER[k - 2]}", i)
                nc.scalar.activation(osum[k % 2][:], banks[:, ATTN, :], ACT.Copy).then_inc(evac.sem, 1)

            def exps(u, i):
                c = u[0]
                before(act, pv, f"c{c}", i)
                before(act, dsum if u in DVE_SUMS else psum, unit(u), i)
                for n, (b0, b1) in enumerate(parts(c)):
                    after(act, shifted, f"{unit(u)}.{n}", i)
                    w = min(b1 * BANK, width(c)) - b0 * BANK
                    src = banks[:, RING[u] + b0:RING[u] + b1, :].rearrange("p b n -> p (b n)")
                    nc.scalar.activation(probs[u][:, b0 * BANK:b0 * BANK + w], src[:, 0:w], ACT.Exp, scale=DH ** -0.5).then_inc(exped.sem, 1)

            def pair(i, r, carry=True, more=True):
                if carry:
                    evacuate(2, i - 1)
                if more:
                    hi("k", 0, i + 1, 1 - r)
                exps((3, 0), i)
                exps((1, 0), i)
                if carry:
                    evacuate(0, i - 1)
                if more:
                    hi("k", 1, i + 1, 1 - r)
                    hi("q", 0, i + 1, 1 - r)
                exps((3, 1), i)
                exps((1, 1), i)
                if more:
                    hi("q", 1, i + 1, 1 - r)
                evacuate(3, i)
                exps((2, 0), i)
                exps((2, 1), i)
                if more:
                    values(0, i + 1, 1 - r)
                    values(1, i + 1, 1 - r)
                exps((0, 0), i)
                exps((0, 1), i)
                evacuate(1, i)

            for name in HALVES:
                hi(name[0], int(name[1]), 0, 0)
            values(0, 0, 0)
            values(1, 0, 0)
            pair(0, 0, carry=False)
            with act.Fori(0, TURNS // 2 - 1) as i2:
                pair(i2 * 2 + 1, 1)
                pair(i2 * 2 + 2, 0)
            pair(TURNS - 1, 1, more=False)
            evacuate(2, TURNS - 1)
            evacuate(0, TURNS - 1)

            copy_transposed(pd, "ln1", 0)
            with act.Fori(0, CHUNKS - 1) as t:
                silus(pd, t)
                copy_transposed(pd, "ln1", t + 1)
            silus(pd, CHUNKS - 1)

        @block.vector
        def _(dve):
            give_credits(dve, "vector")
            steps = Steps(dve, dve_step)
            nc.vector.memset(ones64[:], 1.0).then_inc(consts, 1)
            nc.vector.memset(ones_row[:], 1.0).then_inc(consts, 1)
            nc.vector.memset(bvx, 1.0).then_inc(consts, 1)
            dve.wait_ge(consts, 3)
            nc.vector.tensor_scalar(minus1[:], bvx[:, 0, :], -1.0, None, ALU.mult).then_inc(consts, 1)
            for u in UNITS:
                nc.vector.tensor_scalar(maxrows[u][:, 0:P], bvx[:, 0, :], 0.0, None, ALU.mult).then_inc(consts, 1)
                nc.vector.tensor_scalar(maxrows[u][:, P:QC], bvx[:, 0, :], 0.0, None, ALU.mult).then_inc(consts, 1)
            dve.wait_ge(consts, 4 + 2 * len(UNITS))
            dve.wait_ge(ints_loaded, 16 * 3)
            nc.vector.tensor_copy(wff[:], iload[:, 0:2 * HID].rearrange("p (j n) -> p j n", n=P)).then_inc(weights_ready, 1)
            nc.vector.tensor_copy(wdn[:], iload[:, 2 * HID:3 * HID].rearrange("p (j n) -> p j n", n=P)).then_inc(weights_ready, 1)

            def statistics(t, ln, turn, at):
                before(dve, t.rstd[ln], "r", turn)
                if ln == "ln2":
                    after(dve, t.x1, "x", turn)
                for k in range(CT):
                    nc.vector.bn_stats(stats[ln][:, k, :], xres[:, bass.ds(at + k * D, D)]).then_inc(t.stat[ln].sem, 1)
                after(dve, t.stat[ln], f"s{CT - 1}", turn)
                dve.sem_inc(idle, 1)
                for k in range(CT):
                    nc.vector.bn_aggr(mv[ln][:, k, :], stats[ln][:, k, :]).then_inc(t.stat[ln].sem, 1)

            def layernorm(t, ln, turn, at):
                before(dve, t.tr[ln], "t", turn)
                after(dve, t.rstd[ln], "r", turn)
                for k in range(CT):
                    last = nc.vector.tensor_scalar(xn[ln][:, k, :], xres[:, bass.ds(at + k * D, D)], mv[ln][:, k, 0:1],
                                                   rstd[ln][:, k:k + 1], ALU.subtract, ALU.mult)
                last.then_inc(t.norm[ln].sem, 1)

            def low(t, turn):
                after(dve, t.copied["ln1"], "c", turn)
                nc.vector.tensor_tensor(xth[:, 1, :], banks[:, T_BANK["ln1"], :], xth[:, 0, :], ALU.subtract).then_inc(t.xlo.sem, 1)

            def gate(t, turn):
                for j in range(HB):
                    after(dve, t.silu, f"g{j}", turn)
                    after(dve, t.gu, f"u{j}", turn)
                    before(dve, t.down, "d", turn)
                    nc.vector.tensor_tensor(hidden[:, j, :], gated[:, j, :], banks[:, 1 + HB + j, :], ALU.mult).then_inc(t.hid.sem, 1)

            def residual(t, turn, at):
                after(dve, t.down, "d", turn)
                here = xres[:, bass.ds(at, CT * D)]
                nc.vector.scalar_tensor_tensor(out=here, in0=banks[:, T_BANK["ln1"], :], scalar=0.5 * FS * FS, in1=here,
                                               op0=ALU.mult, op1=ALU.add).then_inc(t.x1.sem, 1)

            def h_low(turn):
                after(dve, pa.hhi, "h", turn)
                before(dve, pa.hstore, "h", turn)
                nc.vector.scalar_tensor_tensor(out=hch[:, 1, :], in0=banks[:, T_BANK["ln2"], :], scalar=b2_sb[:], in1=hch[:, 0, :],
                                               op0=ALU.add, op1=ALU.subtract).then_inc(pa.hlo.sem, 1)

            dve.wait_ge(x_loaded, 16 * 2)
            statistics(pa, "ln1", 0, 0)
            layernorm(pa, "ln1", 0, 0)
            statistics(pa, "ln1", 1, CH)
            low(pa, 0)
            layernorm(pa, "ln1", 1, CH)
            dve.wait_ge(loaded, 16 * 8)
            for g in range(PAIRS):
                nc.vector.tensor_scalar(bvx[:, g, :], bvx[:, g, :], bv_sb[:, g:g + 1], None, ALU.mult).then_inc(bvx_ready, 1)
            gate(pa, 0)
            low(pa, 1)
            residual(pa, 0, 0)
            for k in range(WPARTS):
                dve.wait_ge(w_hi, k + 1)
                dve.wait_ge(wq_loaded, 16 * 2 * WPARTS)
                nc.vector.tensor_tensor(wsplit[k][:, :, :, 1, :], wload[k], wsplit[k][:, :, :, 0, :], ALU.subtract).then_inc(w_lo, 1)
            with dve.Fori(1, CHUNKS - 1) as t:
                at_last, at, at_next = dve.snap((t - 1) * CH), dve.snap(t * CH), dve.snap((t + 1) * CH)
                statistics(pa, "ln2", t - 1, at_last)
                statistics(pa, "ln1", t + 1, at_next)
                layernorm(pa, "ln2", t - 1, at_last)
                layernorm(pa, "ln1", t + 1, at_next)
                gate(pa, t)
                low(pa, t + 1)
                residual(pa, t, at)
                h_low(t - 1)
            t = CHUNKS - 1
            statistics(pa, "ln2", t - 1, (t - 1) * CH)
            layernorm(pa, "ln2", t - 1, (t - 1) * CH)
            gate(pa, t)
            residual(pa, t, t * CH)
            h_low(t - 1)
            statistics(pa, "ln2", t, t * CH)
            layernorm(pa, "ln2", t, t * CH)
            h_low(t)
            after(dve, pa.biased, "b", CHUNKS - 1)

            def lo(kind, j, n, r):
                name, dst = f"{kind}{j}", qt if kind == "q" else kt
                cols = slice(j * BANK, (j + 1) * BANK)
                after(dve, hi_done, name, n)
                nc.vector.scalar_tensor_tensor(out=dst[:, 1, cols], in0=banks[:, PROJ[name], :], in1=dst[:, 0, cols],
                                               scalar=bslot[r][:, 0:1] if kind == "q" else bslot[r][:, 1:2],
                                               op0=ALU.add, op1=ALU.subtract).then_inc(lo_done.sem, 1)

            def block_max(u, i):
                c, acc, b0 = u[0], blockmax[u], RING[u]
                last_bank = banks[:, b0 + c, :]
                used_by(dve, gmax, u, i)
                if c:
                    after(dve, scores, unit(u) + "a", i)
                    steps.mark(nc.vector.tensor_reduce(acc[:], banks[:, b0:b0 + c, :].rearrange("p b (s q) -> p q b s", s=2), AX.XY, ALU.max))
                after(dve, scores, unit(u) + "b", i)
                if c:
                    steps.wait()
                    steps.mark(nc.vector.tensor_tensor(acc[:], last_bank[:, 0:QC], acc[:], ALU.max))
                else:
                    steps.mark(nc.vector.tensor_copy(acc[:], last_bank[:, 0:QC]))
                partial = pieces(c)[2 * c + 1:]
                for n, (_, col, w, q0) in enumerate(partial):
                    steps.wait()
                    col -= c * BANK
                    m = nc.vector.tensor_tensor(acc[:, q0:q0 + w], last_bank[:, col:col + w], acc[:, q0:q0 + w], ALU.max)
                    if n == len(partial) - 1:
                        m.then_inc(maxed.sem, 1)
                    else:
                        steps.mark(m)

            def max_rows(u, i):
                before(dve, shifted, f"{unit(u)}.{len(parts(u[0])) - 1}", i)
                after(dve, gmax, unit(u), i)
                steps.mark(nc.vector.tensor_copy(maxrows[u][0:1, :], rowmax[u][0:1, :]))
                steps.wait()
                nc.vector.tensor_tensor(maxrows[u][32:33, :], rowmax[u][0:1, :], maxrows[u][0:1, :], ALU.subtract).then_inc(rows.sem, 1)

            def key_sum(u, i):
                c, pr, acc = u[0], probs[u], keysum[u]
                after(dve, exped, f"{unit(u)}.{len(parts(c)) - 1}", i)
                before(dve, pv, f"c{c}", i)
                full = 2 * c + 1
                steps.mark(nc.vector.tensor_reduce(acc[:], pr[:, 0:full * QC].rearrange("p (s q) -> p q s", s=full), AX.X, ALU.add))
                partial = pieces(c)[full:]
                for n, (_, col, w, q0) in enumerate(partial):
                    steps.wait()
                    add = nc.vector.tensor_tensor(acc[:, q0:q0 + w], acc[:, q0:q0 + w], pr[:, col:col + w], ALU.add)
                    if n == len(partial) - 1:
                        add.then_inc(dsum.sem, 1)
                    else:
                        steps.mark(add)

            def normalise(c, i, r):
                k = CORDER.index(c)
                after(dve, evac, f"c{c}", i)
                if k:
                    after(dve, normed, f"c{CORDER[k - 1]}", i)
                else:
                    before(dve, normed, f"c{CORDER[-1]}", i)
                steps.mark(nc.vector.reciprocal(rsum[:], osum[k % 2][:, QC:2 * QC]))
                steps.wait()
                nc.vector.tensor_tensor(attn[r][:, c * QC:(c + 1) * QC], osum[k % 2][:, 0:QC], rsum[:], ALU.mult).then_inc(normed.sem, 1)

            def add_output(j, i, at):
                if j == 0:
                    before(dve, wo_added, "o1", i)
                after(dve, wo_done, f"o{j}", i)
                here = xres[:, bass.ds(at + j * BANK, BANK)]
                nc.vector.tensor_tensor(here, banks[:, 2 + j, :], here, ALU.add).then_inc(wo_added.sem, 1)

            def pair(i, r, carry=True, more=True):
                steps.begin(i)
                block_max((3, 0), i)
                block_max((1, 0), i)
                max_rows((3, 0), i)
                if carry:
                    normalise(2, i - 1, 1 - r)
                max_rows((1, 0), i)
                if more:
                    lo("k", 0, i + 1, 1 - r)
                block_max((3, 1), i)
                block_max((1, 1), i)
                max_rows((3, 1), i)
                if carry:
                    normalise(0, i - 1, 1 - r)
                max_rows((1, 1), i)
                if more:
                    lo("k", 1, i + 1, 1 - r)
                    lo("q", 0, i + 1, 1 - r)
                key_sum((3, 0), i)
                block_max((2, 0), i)
                key_sum((3, 1), i)
                block_max((2, 1), i)
                max_rows((2, 0), i)
                if more:
                    lo("q", 1, i + 1, 1 - r)
                max_rows((2, 1), i)
                normalise(3, i, r)
                block_max((0, 0), i)
                block_max((0, 1), i)
                max_rows((0, 0), i)
                max_rows((0, 1), i)
                if carry:
                    at = dve.snap(((i - 1) // PAIRS) * N) if not isinstance(i, int) else ((i - 1) // PAIRS) * N
                    add_output(0, i - 1, at)
                    add_output(1, i - 1, at)
                normalise(1, i, r)
                steps.end()

            for name in HALVES:
                lo(name[0], int(name[1]), 0, 0)
            pair(0, 0, carry=False)
            with dve.Fori(0, TURNS // 2 - 1) as i2:
                pair(i2 * 2 + 1, 1)
                pair(i2 * 2 + 2, 0)
            pair(TURNS - 1, 1, more=False)
            steps.begin(TURNS)
            normalise(2, TURNS - 1, 1)
            normalise(0, TURNS - 1, 1)
            add_output(0, TURNS - 1, (BATCH - 1) * N)
            add_output(1, TURNS - 1, (BATCH - 1) * N)

            after(dve, wo_added, "o1", TURNS - 1)
            statistics(pd, "ln1", 0, 0)
            layernorm(pd, "ln1", 0, 0)
            low(pd, 0)
            with dve.Fori(0, CHUNKS - 1) as t:
                at, at_next = dve.snap(t * CH), dve.snap((t + 1) * CH)
                statistics(pd, "ln1", t + 1, at_next)
                layernorm(pd, "ln1", t + 1, at_next)
                gate(pd, t)
                low(pd, t + 1)
                residual(pd, t, at)
            gate(pd, CHUNKS - 1)
            residual(pd, CHUNKS - 1, (CHUNKS - 1) * CH)

        @block.tensor
        def _(pe):
            give_credits(pe, "tensor")
            mm = nc.tensor.matmul

            def transposed(t, ln, turn):
                after(pe, t.norm[ln], "n", turn)
                for k in range(CT):
                    last = nc.tensor.transpose(banks[:, T_BANK[ln], k * P:(k + 1) * P], xn[ln][:, k, :], ident[:])
                last.then_inc(t.tr[ln].sem, 1)

            def gate_up(t, turn):
                after(pe, t.xlo, "l", turn)
                for j in range(2 * HB):
                    if j < HB:
                        before(pe, t.silu, f"g{j}", turn)
                    else:
                        before(pe, t.hid, f"h{j - HB}", turn)
                    mm(banks[:, 1 + j, :], wff[:, j, :], xth[:, 0, :], start=True, stop=False)
                    mm(banks[:, 1 + j, :], wff[:, j, :], xth[:, 1, :], start=False, stop=True).then_inc(t.gu.sem, 1)

            def down(t, turn, more=True):
                after(pe, t.hid, f"h{HB - 1}", turn)
                after(pe, t.xlo, "l", turn + 1 if more else turn)
                for k in range(CT):
                    for j in range(HB):
                        last = mm(banks[:, T_BANK["ln1"], k * P:(k + 1) * P], hidden[:, j, k * P:(k + 1) * P], wdn[:, j, :],
                                  start=(j == 0), stop=(j == HB - 1))
                last.then_inc(t.down.sem, 1)

            def mlp1(turn):
                after(pe, pa.copied["ln2"], "c", turn)
                mm(banks[:, T_BANK["ln2"], :], w1_sb[:], x2t, start=True, stop=True).then_inc(pa.m1.sem, 1)

            def mlp2(turn):
                after(pe, pa.y1, "y", turn)
                mm(banks[:, T_BANK["ln2"], :], w2_sb[:], y1, start=True, stop=True).then_inc(pa.m2.sem, 1)

            pe.wait_ge(gp_const, 6)
            transposed(pa, "ln1", 0)
            pe.wait_ge(weights_ready, 2)
            gate_up(pa, 0)
            transposed(pa, "ln1", 1)
            pe.wait_ge(loaded, 16 * 8)
            pe.wait_ge(bvx_ready, PAIRS)
            for g in range(PAIRS):
                mm(banks[:, WORK, 0:P], bvx[:, g, :], wo_sb[:, g, :], start=(g == 0), stop=False)
            mm(banks[:, WORK, 0:P], ones_row[:], bo_row[:], start=False, stop=True).then_inc(bo_done, 1)
            down(pa, 0)
            pe.wait_ge(bo_done, 2)
            with pe.Fori(1, CHUNKS - 1) as t:
                gate_up(pa, t)
                before(pe, pa.hlo, "h", t - 1)
                transposed(pa, "ln2", t - 1)
                before(pe, pa.x1, "x", t)
                transposed(pa, "ln1", t + 1)
                mlp1(t - 1)
                down(pa, t)
                mlp2(t - 1)
            t = CHUNKS - 1
            gate_up(pa, t)
            before(pe, pa.hlo, "h", t - 1)
            transposed(pa, "ln2", t - 1)
            mlp1(t - 1)
            down(pa, t, more=False)
            mlp2(t - 1)
            before(pe, pa.hlo, "h", t)
            transposed(pa, "ln2", t)
            mlp1(t)
            mlp2(t)
            pe.wait_ge(consts, 4 + 2 * len(UNITS))

            def project(name, n, r):
                kind, j = name[0], int(name[1])
                i = n - 1
                if name == "k0":
                    after(pe, slots, "b", n)
                    before(pe, lo_done, "q1", n)
                elif name == "k1":
                    after(pe, lo_done, "k0", n)
                elif name == "q0":
                    if isinstance(n, int) and n < 2:
                        before(pe, lo_done, "q0", n)
                    else:
                        after(pe, evac, "c0", i - 1)
                elif name == "q1":
                    after(pe, lo_done, "k1", n)
                elif not (isinstance(n, int) and n == 0):
                    after(pe, exped, "2B.0" if name == "v0" else "2B.1", i)
                bank = banks[:, PROJ[name], :]
                w = wslot[r][:, "qkv".index(kind)]
                if kind != "v":
                    toks = slice(j * BANK, (j + 1) * BANK)
                    mm(bank, w[:, 0, :], hb[r][:, 0, toks], start=True, stop=False)
                    mm(bank, w[:, 0, :], hb[r][:, 1, toks], start=False, stop=False)
                    last = mm(bank, w[:, 1, :], hb[r][:, 0, toks], start=False, stop=True)
                else:
                    for m in range(4):
                        toks = slice((4 * j + m) * P, (4 * j + m + 1) * P)
                        dst = bank[:, m * P:(m + 1) * P]
                        mm(dst, hb[r][:, 0, toks], w[:, 0, :], start=True, stop=False)
                        mm(dst, hb[r][:, 0, toks], w[:, 1, :], start=False, stop=False)
                        last = mm(dst, hb[r][:, 1, toks], w[:, 0, :], start=False, stop=True)
                last.then_inc(proj.sem, 1)

            def freed(u, b, i):
                bank, k = RING[u] + b, UNITS.index(u)
                if k < 2 and bank >= 2:
                    if bank >= 4:
                        after(pe, v_done, f"v{bank - 4}", i)
                    elif not (isinstance(i, int) and i == 0):
                        after(pe, wo_added, f"o{bank - 2}", i - 2)
                    return
                earlier = [(v, after) for v in UNITS[:k][::-1]] + [(v, before) for v in UNITS[::-1]]
                for v, when in earlier:
                    if RING[v] <= bank <= RING[v] + v[0]:
                        return when(pe, exped, f"{unit(v)}.{(bank - RING[v]) // 2}", i)

            def score(u, i, r):
                c, h = u
                if u == UNITS[0]:
                    after(pe, stacks, "qB1", i)
                for kb, col, w, q0 in pieces(c):
                    b = col // BANK
                    first = col % BANK == 0
                    if first:
                        if b == c and c:
                            last.then_inc(scores.sem, 1)
                        freed(u, b, i)
                    dst = banks[:, RING[u] + b, col % BANK:col % BANK + w]
                    qcols = slice(c * QC + q0, c * QC + q0 + w)
                    m0 = c * QC + q0 - (kb * P - WINDOW)
                    edge = min(P - m0, w) if m0 < P else 0
                    mm(dst, ks[r][h][:, 0, kb * P:(kb + 1) * P], qs[r][h][:, qcols], start=first, stop=False, skip_group_check=True)
                    last = mm(dst, ks[r][h][:, 1, kb * P:(kb + 1) * P], qs[r][h][:, qcols], start=False, stop=not edge, skip_group_check=True)
                    if edge:
                        last = mm(dst[:, 0:edge], ident16[:], mask16[:, m0:m0 + edge], start=False, stop=True, skip_group_check=True)
                last.then_inc(scores.sem, 1)

            def shift(u, i):
                c = u[0]
                after(pe, rows, unit(u), i)
                for b0, b1 in parts(c):
                    for b in range(b0, b1):
                        bank = banks[:, RING[u] + b, :]
                        here = [(col - b * BANK, w, q0) for _, col, w, q0 in pieces(c) if col // BANK == b]
                        if len(here) == 2 and here[1][1] == QC:
                            last = mm(bank.rearrange("p (s q) -> p s q", s=2), minus1[:], maxrows[u][:].unsqueeze(1).to_broadcast([P, 2, QC]),
                                      start=False, stop=True, skip_group_check=True)
                        else:
                            for col, w, q0 in here:
                                last = mm(bank[:, col:col + w], minus1[:], maxrows[u][:, q0:q0 + w], start=False, stop=True, skip_group_check=True)
                    last.then_inc(shifted.sem, 1)

            def attend(c, i, r, more=True):
                k = CORDER.index(c)
                if k:
                    after(pe, evac, f"c{CORDER[k - 1]}", i)
                elif more:
                    after(pe, lo_done, "q0", i + 1)
                else:
                    after(pe, evac, "c0", i - 1)
                if k == 0:
                    after(pe, v_done, "v1", i)
                after(pe, exped, f"{c}B.{len(parts(c)) - 1}", i)
                ps = pieces(c)
                for kb, col, w, q0 in ps:
                    for h in range(2):
                        mm(banks[half(h), ATTN, q0:q0 + w], vs[r][:, kb, half(h)], probs[c, h][:, col:col + w],
                           start=(kb == 0), stop=(kb == ps[-1][0]), skip_group_check=True)
                for h in range(2):
                    after(pe, dsum if (c, h) in DVE_SUMS else psum, unit((c, h)), i)
                    last = mm(banks[half(h), ATTN, QC:2 * QC], ones64[:], keysum[c, h][:], start=True, stop=True, skip_group_check=True)
                last.then_inc(pv.sem, 1)

            def output(j, i, r):
                g = pe.snap(i % PAIRS) if not isinstance(i, int) else i % PAIRS
                after(pe, normed, "c0", i)
                for m in range(4):
                    tile = slice((4 * j + m) * P, (4 * j + m + 1) * P)
                    last = mm(banks[:, 2 + j, m * P:(m + 1) * P], attn[r][:, tile], wo_sb[:, bass.ds(g, 1), :].rearrange("p g n -> p (g n)"),
                              start=True, stop=True)
                last.then_inc(wo_done.sem, 1)

            def pair(i, r, carry=True, more=True):
                score((3, 0), i, r)
                score((1, 0), i, r)
                if carry:
                    attend(2, i - 1, 1 - r)
                if more:
                    project("k0", i + 1, 1 - r)
                shift((3, 0), i)
                shift((1, 0), i)
                score((3, 1), i, r)
                score((1, 1), i, r)
                if carry:
                    attend(0, i - 1, 1 - r)
                if more:
                    project("k1", i + 1, 1 - r)
                    project("q0", i + 1, 1 - r)
                shift((3, 1), i)
                shift((1, 1), i)
                score((2, 0), i, r)
                score((2, 1), i, r)
                if more:
                    project("q1", i + 1, 1 - r)
                attend(3, i, r, more)
                shift((2, 0), i)
                shift((2, 1), i)
                score((0, 0), i, r)
                score((0, 1), i, r)
                if more:
                    project("v0", i + 1, 1 - r)
                    project("v1", i + 1, 1 - r)
                if carry:
                    after(pe, exped, "2A.1", i)
                    output(0, i - 1, 1 - r)
                    after(pe, exped, "2B.0", i)
                    output(1, i - 1, 1 - r)
                shift((0, 0), i)
                shift((0, 1), i)
                attend(1, i, r)

            after(pe, pa.hlo, "h", CHUNKS - 1)
            after(pe, pa.x1, "x", CHUNKS - 1)
            for name in proj.events:
                project(name, 0, 0)
            pair(0, 0, carry=False)
            with pe.Fori(0, TURNS // 2 - 1) as i2:
                pair(i2 * 2 + 1, 1)
                pair(i2 * 2 + 2, 0)
            pair(TURNS - 1, 1, more=False)
            attend(2, TURNS - 1, 1)
            attend(0, TURNS - 1, 1)
            output(0, TURNS - 1, 1)
            output(1, TURNS - 1, 1)

            after(pe, wo_added, "o1", TURNS - 1)
            transposed(pd, "ln1", 0)
            with pe.Fori(0, CHUNKS - 1) as t:
                gate_up(pd, t)
                before(pe, pd.x1, "x", t)
                transposed(pd, "ln1", t + 1)
                down(pd, t)
            gate_up(pd, CHUNKS - 1)
            down(pd, CHUNKS - 1, more=False)


def kernel(L0_attn_x, L0_attn_W1, L0_attn_b1, L0_attn_W2, L0_attn_b2, L0_attn_Wg, L0_attn_bg, L0_attn_Wo, L0_attn_bo,
           L0_ffn_w_gate, L0_ffn_w_up, L0_ffn_w_down):
    import numpy as np
    import concourse.bacc as bacc
    from concourse.bass_utils import run_bass_kernel_spmd

    x = np.asarray(L0_attn_x)
    bg = np.asarray(L0_attn_bg).reshape(3, -1, P)
    arrays = {
        "x": x.reshape(-1, x.shape[-1]),
        "w1t": np.asarray(L0_attn_W1).T, "b1": np.asarray(L0_attn_b1).reshape(-1, 1),
        "w2t": np.asarray(L0_attn_W2).T, "b2": np.asarray(L0_attn_b2).reshape(-1, 1),
        "wqkvt": np.asarray(L0_attn_Wg).T,
        "bqk": bg[0:2].transpose(2, 1, 0).reshape(P, -1), "bv": bg[2].T,
        "wot": np.asarray(L0_attn_Wo).T, "bo": np.asarray(L0_attn_bo).reshape(1, -1),
        "wgatet": np.asarray(L0_ffn_w_gate).T, "wupt": np.asarray(L0_ffn_w_up).T, "wdownt": np.asarray(L0_ffn_w_down).T,
    }
    nc = bacc.Bacc("TRN2", target_bir_lowering=False, num_devices=1)
    feed, args = {}, []
    for name, a in arrays.items():
        feed[f"in_{name}"] = np.ascontiguousarray(a)
        args.append(nc.dram_tensor(f"in_{name}", a.shape, mybir.dt.from_np(a.dtype), kind="ExternalInput").ap())
    out = nc.dram_tensor("y", arrays["x"].shape, F32, kind="ExternalOutput").ap()
    macaron(nc, *args, out)
    r = run_bass_kernel_spmd(nc, [feed], core_ids=[0])
    return r.results[0]["y"].reshape(x.shape)
```

```python
from contextlib import ExitStack

import concourse.bass as bass
from concourse import mybir

F32 = mybir.dt.float32
F32R = mybir.dt.float32r
BF16 = mybir.dt.bfloat16
I32 = mybir.dt.int32
ALU = mybir.AluOpType
ACT = mybir.ActivationFunctionType
AX = mybir.AxisListType
MAX = bass.bass_isa.ReduceOp.max

P = 128
BANK = 512
MASKED = -3.0e38
EPS = 1e-5


class Tally:

    def __init__(self, sem, events, step=1):
        self.sem, self.events, self.step = sem, list(events), step
        self.per_pass = len(self.events) * step

    def after(self, event, turn):
        return (turn + 1) * self.per_pass + (self.events.index(event) + 1) * self.step

    def before(self, event, turn):
        return turn * self.per_pass + (self.events.index(event) + 1) * self.step


def macaron(nc, x, w1t, b1, w2t, b2, wqkvt, bqk, bv, wot, bo, wgatet, wupt, wdownt, out):
    TOK, D = x.shape
    BATCH, N = 4, TOK // 4
    DH, WINDOW = 64, 64
    PAIRS = wot.shape[0] // P
    TURNS = BATCH * PAIRS
    HID = wgatet.shape[1]
    HB = HID // P
    FS = 1.0 / 127.0
    CH = 512
    CHUNKS = TOK // CH
    CT = CH // P
    QC = 256
    assert D == P and N == 1024 and CH == BANK

    UNITS = [(3, 1), (1, 1), (0, 0), (3, 0), (1, 0), (0, 1), (2, 0), (2, 1)]
    RING = {(3, 1): 0, (1, 1): 5, (0, 0): 7, (3, 0): 0, (1, 0): 5, (0, 1): 0, (2, 0): 4, (2, 1): 1}
    ATTN = {0: 2, 1: 5, 2: 7, 3: 7}
    PROJ = {"k0": 4, "k1": 4, "q0": 4, "q1": 3, "v0": 5, "v1": 6}
    OUT = {"o0": 7, "o1": 1, "o2": 4, "o3": 4}
    BANK_ORDER = {
        0: [("3B", 0), ("3A", 0), ("0B", 0)],
        1: [("3B", 0), ("3A", 0), ("o1", 1), ("2B", 0)],
        2: [("3B", 0), ("3A", 0), ("c0", 1), ("2B", 0)],
        3: [("3B", 0), ("3A", 0), ("q1", -1), ("2B", 0)],
        4: [("k0", -1), ("q0", -1), ("k1", -1), ("o3", 1), ("2A", 0), ("o2", 1)],
        5: [("1B", 0), ("1A", 0), ("2A", 0), ("v0", -1), ("c1", 0)],
        6: [("1B", 0), ("1A", 0), ("2A", 0), ("v1", -1)],
        7: [("c2", 1), ("0A", 0), ("c3", 0), ("o0", 1)],
    }
    SHARED = 4
    T_BANK = {"ln1": 1, "ln2": 7}
    DOWN = 0
    WORK = 7

    def pieces(c):
        full = [(kb, kb * QC, QC, 0) for kb in range(2 * c + 1)]
        part = [(2 * c + 1, (2 * c + 1) * QC, QC - WINDOW, WINDOW)]
        last = [(2 * c + 2, (2 * c + 2) * QC - WINDOW, WINDOW, QC - WINDOW)] if 2 * c + 2 < N // P else []
        return full + part + last

    def width(c):
        return sum(w for _, _, w, _ in pieces(c))

    def parts(c):
        return [(b, min(b + 2, c + 1)) for b in range(0, c + 1, 2)]

    def unit(u):
        return f"{u[0]}{'AB'[u[1]]}"

    with ExitStack() as ctx:
        def sb(name, shape, dt=F32):
            return ctx.enter_context(nc.sbuf_tensor(name, shape, dt))

        def sem(name):
            return ctx.enter_context(nc.semaphore(name))

        ident = sb("ident", [P, P])
        ident16 = sb("ident16", [P, P], BF16)
        mask16 = sb("mask16", [P, P], BF16)
        ones = sb("ones", [P, 1])
        minus1 = sb("minus1", [P, P], F32R)
        minus_ident = sb("minus_ident", [P, P], F32R)
        w1_sb = sb("w1_sb", [P, P])
        w2_sb = sb("w2_sb", [P, P])
        b1_sb = sb("b1_sb", [P, 1])
        b2_sb = sb("b2_sb", [P, 1])
        bqk_sb = sb("bqk_sb", [P, PAIRS, 2])
        bv_sb = sb("bv_sb", [P, PAIRS])
        bo_row = sb("bo_row", [1, P])
        ones_row = sb("ones_row", [1, P])
        bo_all = sb("bo_all", [P, P])
        wo_sb = sb("wo_sb", [P, PAIRS, P])
        wff = sb("wff", [P, 2 * HB, P], F32R)
        wdn = sb("wdn", [P, HB, P])
        xres = sb("xres", [P, TOK // P * D])
        probs = {(c, h): sb(f"probs{c}{h}", [P, (c + 1) * BANK]) for c in range(4) for h in range(2)}
        blockmax_of = [sb(f"blockmax{k}", [P, QC]) for k in range(SHARED)]
        rowmax_of = [sb(f"rowmax{k}", [P, QC]) for k in range(SHARED)]
        MAX_ORDER, PAR_ORDER = [(3, 1), (1, 1), (0, 0), (3, 0), (1, 0), (0, 1), (2, 0), (2, 1)], [(3, 1), (1, 1), (0, 0), (3, 0), (1, 0), (0, 1), (2, 0), (2, 1)]
        blockmax = {u: blockmax_of[k % SHARED] for k, u in enumerate(MAX_ORDER)}
        rowmax = {u: rowmax_of[k % SHARED] for k, u in enumerate(PAR_ORDER)}
        maxrows = {u: sb(f"maxrows{unit(u)}", [P, QC], F32R) for u in UNITS}
        keysum = {u: sb(f"keysum{unit(u)}", [P, QC]) for u in UNITS}
        qs = [[sb(f"qs{r}{h}", [P, N], F32R) for h in range(2)] for r in range(2)]
        ks = [[sb(f"ks{r}{h}", [P, 2, N], F32R) for h in range(2)] for r in range(2)]
        vs = [sb(f"vs{r}", [P, N // P, P]) for r in range(2)]
        kt = sb("kt", [P, 2, N], F32R)
        qt = sb("qt", [P, 2, N], F32R)
        attn = [sb(f"attn{r}", [P, N // QC, QC + 4]) for r in range(2)]
        attn_flat = [a[:].rearrange("p c n -> p (c n)") for a in attn]
        recips = [sb(f"recips{r}", [P, 4, 4]) for r in range(2)]
        hb = [sb(f"hb{r}", [P, 2, N], F32R) for r in range(2)]
        wslot = [sb(f"wslot{r}", [P, 3, 2, P], F32R) for r in range(2)]
        woslot = [sb(f"woslot{r}", [P, 2, P]) for r in range(2)]
        bslot = [sb(f"bslot{r}", [P, 2]) for r in range(2)]
        def tokens(buf, k):
            return buf[:, k * CH:(k + 1) * CH].rearrange("p (k d) -> p k d", d=D)

        LNS = ["ln1", "ln2"]
        xn = {ln: tokens(attn_flat[1], k) for k, ln in enumerate(LNS)}
        stats = {ln: sb(f"stats_{ln}", [P, CT, 6]) for ln in LNS}
        mv = {ln: sb(f"mv_{ln}", [P, CT, 2]) for ln in LNS}
        rstd = {ln: sb(f"rstd_{ln}", [P, CT]) for ln in LNS}
        veps = {ln: sb(f"veps_{ln}", [P, CT]) for ln in LNS}
        mhalf = sb("mhalf", [P, CT])
        xth = qs[0][0][:].rearrange("p (s n) -> p s n", s=2)
        hch = qs[0][1][:].rearrange("p (s n) -> p s n", s=2)
        gated = probs[3, 0][:, 0:HB * CH].rearrange("p (j n) -> p j n", j=HB)
        hidden = probs[3, 1][:, 0:HB * CH].rearrange("p (j n) -> p j n", j=HB)
        x2t = probs[2, 0][:, 0:CH]
        y1 = probs[2, 0][:, CH:2 * CH]
        iload = probs[3, 1][:, 0:3 * HID].bitcast(I32)
        bvx = attn_flat[0][:, 0:PAIRS * P].rearrange("p (g n) -> p g n", n=P)
        WPARTS, WCOLS = PAIRS // 2, 2 * 3 * P
        wload = [b.rearrange("p (g t n) -> p g t n", g=2, t=3) for b in
                 (probs[2, 1][:, 0:WCOLS], probs[2, 1][:, WCOLS:2 * WCOLS], probs[1, 0][:, 0:WCOLS], probs[1, 1][:, 0:WCOLS])]
        wsplit = [ks[k // 2][k % 2][:].rearrange("p s n -> p (s n)")[:, 0:2 * WCOLS].rearrange("p (g t s n) -> p g t s n", g=2, t=3, s=2)
                  for k in range(WPARTS)]

        banks = ctx.enter_context(nc.psum_tensor("banks", [P, 8, BANK], F32))

        h_dram = nc.dram_tensor("h_scratch", [2, P, TOK], F32, kind="Internal").ap()
        w_dram = nc.dram_tensor("w_scratch", [P, PAIRS, 3 * 2 * P], F32, kind="Internal").ap()

        ints_loaded = sem("ints_loaded")
        x_loaded = sem("x_loaded")
        loaded = sem("loaded")
        wq_loaded = sem("wq_loaded")
        consts = sem("consts")
        weights_ready = sem("weights_ready")
        gp_const = sem("gp_const")
        bvx_ready = sem("bvx_ready")
        bo_done = sem("bo_done")
        w_hi = sem("w_hi")
        w_lo = sem("w_lo")
        w_stored = sem("w_stored")
        stored = sem("stored")
        idle = sem("idle")

        class Phase:
            pass

        def phase(name, lns):
            t = Phase()
            T = lambda n, ev, step=1: Tally(sem(f"{name}_{n}"), ev, step)
            t.stat = {ln: T(f"stat_{ln}", [f"{s}{k}" for s in "sa" for k in range(CT)]) for ln in lns}
            t.rstd = {ln: T(f"rstd_{ln}", ["e", "r"]) for ln in lns}
            t.norm = {ln: T(f"norm_{ln}", ["n"]) for ln in lns}
            t.tr = {ln: T(f"tr_{ln}", ["t"]) for ln in lns}
            t.copied = {ln: T(f"copied_{ln}", ["c"]) for ln in lns}
            t.xlo = T("xlo", ["l"])
            t.gu = T("gu", [f"g{j}" for j in range(HB)] + [f"u{j}" for j in range(HB)])
            t.silu = T("silu", [f"g{j}" for j in range(HB)])
            t.hid = T("hid", [f"h{j}" for j in range(HB)])
            t.down = T("down", ["d"])
            t.x1 = T("x1", ["x"])
            t.biased = T("biased", ["b"])
            t.m1 = T("m1", ["m"])
            t.y1 = T("y1", ["y"])
            t.m2 = T("m2", ["m"])
            t.hhi = T("hhi", ["h"])
            t.hlo = T("hlo", ["h"])
            t.hstore = T("hstore", ["h"], 16)
            return t

        pa, pd = phase("a", LNS), phase("d", LNS[:1])

        T = lambda n, ev, step=1: Tally(sem(n), ev, step)
        score_events = [e for u in UNITS for e in ([unit(u) + "a"] if u[0] else []) + [unit(u) + "b"]]
        SHIFT_ORDER, EXP_ORDER = [(3, 1), (1, 1), (0, 0), (3, 0), (1, 0), (2, 0), (0, 1), (2, 1)], [(3, 1), (1, 1), (3, 0), (1, 0), (0, 0), (2, 0), (2, 1), (0, 1)]
        pieces_of = lambda order: [f"{unit(u)}.{n}" for u in order for n in range(len(parts(u[0])))]
        scores = T("scores", score_events)
        maxed = T("maxed", [unit(u) for u in MAX_ORDER])
        gmax = T("gmax", [unit(u) for u in PAR_ORDER])
        row_hi = T("row_hi", [unit(u) for u in [(3, 1), (1, 1), (0, 0), (3, 0), (1, 0), (0, 1), (2, 0), (2, 1)]])
        rows = T("rows", [unit(u) for u in [(3, 1), (1, 1), (0, 0), (3, 0), (1, 0), (2, 0), (0, 1), (2, 1)]])
        shifted = T("shifted", pieces_of(SHIFT_ORDER))
        exped = T("exped", pieces_of(EXP_ORDER))
        DVE_SUMS = [(1, 1), (3, 0), (2, 0)]
        POOL_SUMS = [(3, 1), (1, 0), (2, 1), (0, 1), (0, 0)]
        dsum = T("dsum", [unit(u) for u in DVE_SUMS])
        psum = T("psum_", [unit(u) for u in POOL_SUMS])
        CORDER = [3, 1, 2, 0]
        pv = T("pv", [f"c{c}" for c in CORDER])
        evac = T("evac", ['c3', 'c1', 'c2', 'c0'])
        recip = T("recip", ['c3', 'c1', 'c0', 'c2'])
        proj = T("proj", ['k0', 'q0', 'k1', 'q1', 'v0', 'v1'])
        hi_done = T("hi_done", ['k0', 'q0', 'k1', 'q1'])
        split = T("split", ['k0', 'q0', 'k1', 'q1'])
        lo_done = T("lo_done", ['k0', 'q0', 'k1', 'q1'])
        v_done = T("v_done", ['v0', 'v1'])
        stacks = T("stacks", [f"{t}{h}{s}" for t in "kq" for h in "AB" for s in "01"], 16)
        slots = T("slots", ["h", "w", "b"], 16)
        wo_done = T("wo_done", ['o3', 'o1', 'o0', 'o2'])
        woslots = [T(f"woslots{r}", ["wA", "wB"], 16) for r in range(2)]
        wo_added = T("wo_added", ['o3', 'o1', 'o0', 'o2'])
        dve_step = T("dve_step", range(33))
        pool_step = T("pool_step", range(18))

        credits = {
            "sync": [stacks, slots, *woslots], "vector": [maxed, rows, dsum, recip, wo_added, dve_step],
            "scalar": [row_hi, exped, hi_done, lo_done, v_done, evac], "tensor": [scores, shifted, pv, proj, split, wo_done],
            "gpsimd": [gmax, psum, pool_step],
        }
        for t in (pa, pd):
            credits["sync"] += [t.hstore]
            credits["vector"] += [*t.stat.values(), *t.norm.values(), t.xlo, t.hid, t.x1, t.hlo]
            credits["gpsimd"] += [*t.rstd.values(), t.biased]
            credits["tensor"] += [*t.tr.values(), t.gu, t.down, t.m1, t.m2]
            credits["scalar"] += [*t.copied.values(), t.silu, t.y1, t.hhi]

        def give_credits(eng, name):
            for t in credits[name]:
                eng.sem_inc(t.sem, t.per_pass)

        def used_by(eng, tally, order, u, i):
            k = order.index(u)
            eng.wait_ge(tally.sem, tally.after(unit(order[k - SHARED]), i) if k >= SHARED else tally.before(unit(order[k - SHARED]), i))

        class Steps:

            def __init__(self, eng, tally):
                self.eng, self.tally = eng, tally

            def begin(self, turn):
                self.turn, self.n = turn, 0

            def mark(self, instruction):
                self.n += 1
                instruction.then_inc(self.tally.sem, 1)

            def wait(self):
                self.eng.wait_ge(self.tally.sem, self.tally.after(self.n - 1, self.turn))

            def end(self):
                left = len(self.tally.events) - self.n
                assert left >= 0, self.n
                if left:
                    self.eng.sem_inc(self.tally.sem, left)

        def half(h):
            return slice(DH * h, DH * h + DH)

        block = ctx.enter_context(nc.Block())

        @block.sync
        def _(sp):
            give_credits(sp, "sync")
            for dst, src in ((iload[:, 0:HID], wgatet), (iload[:, HID:2 * HID], wupt),
                             (iload[:, 2 * HID:3 * HID].rearrange("p (j n) -> p j n", j=HB), wdownt.rearrange("(j p) n -> p j n", p=P))):
                sp.dma_start(dst, src).then_inc(ints_loaded, 16)
            x_src = x.rearrange("(k p) d -> p k d", p=P)
            resident = xres[:].rearrange("p (k d) -> p k d", d=D)
            half_tiles = TOK // P // 2
            for k in range(2):
                tiles = slice(k * half_tiles, (k + 1) * half_tiles)
                sp.dma_start(resident[:, tiles, :], x_src[:, tiles, :]).then_inc(x_loaded, 16)
            for dst, src in (
                (w1_sb[:], w1t), (w2_sb[:], w2t), (b1_sb[:], b1), (b2_sb[:], b2),
                (bqk_sb[:], bqk.rearrange("p (g t) -> p g t", t=2)), (bv_sb[:], bv),
                (wo_sb[:], wot.rearrange("(g p) n -> p g n", p=P)), (bo_row[:], bo),
            ):
                sp.dma_start(dst, src).then_inc(loaded, 16)
            sp.wait_ge(weights_ready, 2)
            wq_src = wqkvt.rearrange("p (t k g n) -> p k g t n", t=3, k=WPARTS, n=P)
            for k in range(WPARTS):
                for g in range(2):
                    sp.dma_start(wload[k][:, g], wq_src[:, k, g]).then_inc(wq_loaded, 16)
            for k in range(WPARTS):
                sp.wait_ge(w_hi, k + 1)
                sp.wait_ge(w_lo, k + 1)
                sp.dma_start(w_dram[:, 2 * k:2 * k + 2, :].rearrange("p g n -> p (g n)"),
                             wsplit[k].rearrange("p g t s n -> p (g t s n)").bitcast(F32)).then_inc(w_stored, 16)
            def store_h(t, at):
                sp.wait_ge(pa.hhi.sem, pa.hhi.after("h", t))
                sp.wait_ge(pa.hlo.sem, pa.hlo.after("h", t))
                sp.dma_start(h_dram[:, :, bass.ds(at, CH)].rearrange("s p n -> p s n"), hch.bitcast(F32)).then_inc(pa.hstore.sem, 16)

            with sp.Fori(0, CHUNKS - 1) as t:
                store_h(t, sp.snap(t * CH))

            def load_slots(n, r):
                h_at = sp.snap((n // PAIRS) * N) if not isinstance(n, int) else 0
                g_at = sp.snap(n % PAIRS) if not isinstance(n, int) else n
                if not (isinstance(n, int) and n == 0):
                    sp.wait_ge(slots.sem, slots.after("b", n - 1))
                if not isinstance(n, int):
                    sp.wait_ge(proj.sem, proj.after("v1", n - 2))
                    sp.wait_ge(lo_done.sem, lo_done.after("q1", n - 2))
                sp.dma_start(hb[r][:].bitcast(F32), h_dram[:, :, bass.ds(h_at, N)].rearrange("s p n -> p s n")).then_inc(slots.sem, 16)
                sp.dma_start(wslot[r][:].bitcast(F32).rearrange("p t s n -> p (t s n)").unsqueeze(1), w_dram[:, bass.ds(g_at, 1), :]).then_inc(slots.sem, 16)
                sp.dma_start(bslot[r][:].unsqueeze(1), bqk_sb[:, bass.ds(g_at, 1), :]).then_inc(slots.sem, 16)

            def stack(n, r):
                sp.wait_ge(hi_done.sem, hi_done.after("k1", n))
                sp.wait_ge(lo_done.sem, lo_done.after("k1", n))
                for h in range(2):
                    for s in range(2):
                        sp.dma_start(ks[r][h][half(s)].bitcast(F32), kt[half(h)].bitcast(F32)).then_inc(stacks.sem, 16)
                sp.wait_ge(hi_done.sem, hi_done.after("q1", n))
                sp.wait_ge(lo_done.sem, lo_done.after("q1", n))
                for h in range(2):
                    for s in range(2):
                        sp.dma_start(qs[r][h][half(s)].bitcast(F32), qt[half(h), s, :].bitcast(F32)).then_inc(stacks.sem, 16)

            def load_output_weights(n, r):
                at = sp.snap((n % PAIRS) * P) if not isinstance(n, int) else (n % PAIRS) * P
                if not (isinstance(n, int) and n < 2):
                    sp.wait_ge(wo_done.sem, wo_done.after("o2", n - 2))
                for h in range(2):
                    sp.dma_start(woslot[r][half(h), h, :], wo_sb[half(h)].rearrange("p g n -> p (g n)")[:, bass.ds(at, P)]).then_inc(woslots[r].sem, 16)

            sp.wait_ge(pa.hstore.sem, pa.hstore.after("h", CHUNKS - 2))
            sp.wait_ge(w_stored, 16 * WPARTS)
            load_slots(0, 0)
            load_slots(1, 1)
            store_h(CHUNKS - 1, (CHUNKS - 1) * CH)
            sp.wait_ge(pa.hstore.sem, pa.hstore.after("h", CHUNKS - 1))
            stack(0, 0)
            load_output_weights(0, 0)
            with sp.Fori(0, TURNS // 2 - 1) as i:
                load_slots(i * 2 + 2, 0)
                stack(i * 2 + 1, 1)
                load_output_weights(i * 2 + 1, 1)
                load_slots(i * 2 + 3, 1)
                stack(i * 2 + 2, 0)
                load_output_weights(i * 2 + 2, 0)
            stack(TURNS - 1, 1)
            load_output_weights(TURNS - 1, 1)

            out_dst = out.rearrange("(k p) d -> p k d", p=P)
            with sp.Fori(0, CHUNKS) as t:
                at = sp.snap(t * CT)
                sp.wait_ge(pd.x1.sem, pd.x1.after("x", t))
                sp.dma_start(out_dst[:, bass.ds(at, CT), :], resident[:, bass.ds(at, CT), :]).then_inc(stored, 16)
            sp.wait_ge(stored, 16 * CHUNKS)

        @block.gpsimd
        def _(pool):
            give_credits(pool, "gpsimd")
            steps = Steps(pool, pool_step)
            nc.gpsimd.memset(ident[:], 0.0).then_inc(gp_const, 1)
            nc.gpsimd.memset(mask16[:], 0.0).then_inc(gp_const, 1)
            nc.gpsimd.memset(mhalf[:], -0.5).then_inc(gp_const, 1)
            pool.wait_ge(gp_const, 3)
            nc.gpsimd.affine_select(out=ident[:], in_=ident[:], compare_op=ALU.not_equal, fill=1.0, base=0,
                                    pattern=[[-1, P]], channel_multiplier=1).then_inc(gp_const, 1)
            nc.gpsimd.affine_select(out=mask16[:], in_=mask16[:], compare_op=ALU.is_ge, fill=MASKED, base=-1,
                                    pattern=[[1, P]], channel_multiplier=-1).then_inc(gp_const, 1)
            pool.wait_ge(gp_const, 5)
            nc.gpsimd.tensor_copy(ident16[:], ident[:]).then_inc(gp_const, 1)
            pool.wait_ge(gp_const, 6)

            def rstd_of(t, ln, turn):
                pool.wait_ge(t.stat[ln].sem, t.stat[ln].after(f"a{CT - 1}", turn))
                pool.sem_inc(idle, 1)
                nc.gpsimd.tensor_scalar(veps[ln][:], mv[ln][:, :, 1], EPS, None, ALU.add).then_inc(t.rstd[ln].sem, 1)
                pool.wait_ge(t.rstd[ln].sem, t.rstd[ln].after("e", turn))
                nc.gpsimd.tensor_tensor(rstd[ln][:], veps[ln][:], mhalf[:], ALU.pow).then_inc(t.rstd[ln].sem, 1)

            def add_bias(turn, at):
                pool.wait_ge(pa.norm["ln2"].sem, pa.norm["ln2"].after("n", turn))
                here = xres[:, bass.ds(at, CT * D)].rearrange("p (k d) -> p k d", d=D)
                nc.gpsimd.tensor_tensor(here, here, bo_all[:].unsqueeze(1).to_broadcast([P, CT, P]), ALU.add).then_inc(pa.biased.sem, 1)

            rstd_of(pa, "ln1", 0)
            rstd_of(pa, "ln1", 1)
            pool.wait_ge(bo_done, 2)
            with pool.Fori(1, CHUNKS - 1) as t:
                at = pool.snap((t - 1) * CH)
                rstd_of(pa, "ln2", t - 1)
                rstd_of(pa, "ln1", t + 1)
                add_bias(t - 1, at)
            for t in range(CHUNKS - 2, CHUNKS):
                rstd_of(pa, "ln2", t)
                add_bias(t, t * CH)

            def row_max(u, i):
                used_by(pool, rows, PAR_ORDER, u, i)
                pool.wait_ge(maxed.sem, maxed.after(unit(u), i))
                pool.sem_inc(idle, 1)
                nc.gpsimd.partition_all_reduce(rowmax[u][:], blockmax[u][:], P, MAX).then_inc(gmax.sem, 1)

            def key_sum(u, i):
                c, pr, acc = u[0], probs[u], keysum[u]
                pool.wait_ge(exped.sem, exped.after(f"{unit(u)}.{len(parts(c)) - 1}", i))
                pool.wait_ge(pv.sem, pv.before(f"c{c}", i))
                if c == 0:
                    pool.sem_inc(idle, 1)
                    steps.mark(nc.gpsimd.tensor_copy(acc[:, 0:WINDOW], pr[:, 0:WINDOW]))
                rest = pieces(c)[1:]
                for n, (_, col, w, q0) in enumerate(rest):
                    if n:
                        steps.wait()
                    src = acc if n else pr
                    add = nc.gpsimd.tensor_tensor(acc[:, q0:q0 + w], src[:, q0:q0 + w], pr[:, col:col + w], ALU.add)
                    if n == len(rest) - 1:
                        add.then_inc(psum.sem, 1)
                    else:
                        steps.mark(add)

            def pair(i, carry=True, more=True):
                steps.begin(i)
                if carry:
                    key_sum((0, 1), i - 1)
                row_max((3, 1), i)
                row_max((1, 1), i)
                row_max((0, 0), i)
                if carry:
                    key_sum((0, 0), i - 1)
                row_max((3, 0), i)
                row_max((1, 0), i)
                key_sum((3, 1), i)
                row_max((0, 1), i)
                row_max((2, 0), i)
                key_sum((1, 0), i)
                row_max((2, 1), i)
                key_sum((2, 1), i)
                steps.end()

            pair(0, carry=False)
            with pool.Fori(1, TURNS - 1) as i:
                pair(i)
            pair(TURNS - 1, more=False)
            steps.begin(TURNS)
            key_sum((0, 1), TURNS - 1)
            key_sum((0, 0), TURNS - 1)

            rstd_of(pd, "ln1", 0)
            with pool.Fori(1, CHUNKS) as t:
                rstd_of(pd, "ln1", t)

        @block.scalar
        def _(act):
            give_credits(act, "scalar")

            def copy_transposed(t, ln, turn):
                act.wait_ge(t.tr[ln].sem, t.tr[ln].after("t", turn))
                if ln == "ln1":
                    act.wait_ge(t.gu.sem, t.gu.before(f"u{HB - 1}", turn))
                    nc.scalar.activation(xth[:, 0, :], banks[:, T_BANK[ln], :], ACT.Copy).then_inc(t.copied[ln].sem, 1)
                else:
                    act.wait_ge(t.m1.sem, t.m1.before("m", turn))
                    nc.scalar.activation(x2t, banks[:, T_BANK[ln], :], ACT.Copy).then_inc(t.copied[ln].sem, 1)

            def silus(t, turn):
                for j in range(HB):
                    act.wait_ge(t.gu.sem, t.gu.after(f"g{j}", turn))
                    act.wait_ge(t.hid.sem, t.hid.before(f"h{j}", turn))
                    nc.scalar.activation(gated[:, j, :], banks[:, 1 + j, :], ACT.Silu, scale=FS).then_inc(t.silu.sem, 1)

            def mlp(turn):
                act.wait_ge(pa.m1.sem, pa.m1.after("m", turn))
                nc.scalar.activation(y1, banks[:, T_BANK["ln2"], :], ACT.Silu, bias=b1_sb[:]).then_inc(pa.y1.sem, 1)
                act.wait_ge(pa.m2.sem, pa.m2.after("m", turn))
                act.wait_ge(pa.hstore.sem, pa.hstore.before("h", turn))
                nc.scalar.activation(hch[:, 0, :], banks[:, T_BANK["ln2"], :], ACT.Identity, bias=b2_sb[:]).then_inc(pa.hhi.sem, 1)

            copy_transposed(pa, "ln1", 0)
            silus(pa, 0)
            copy_transposed(pa, "ln1", 1)
            act.wait_ge(bo_done, 1)
            nc.scalar.activation(bo_all[:], banks[:, WORK, 0:P], ACT.Copy).then_inc(bo_done, 1)
            for k in range(WPARTS):
                act.wait_ge(wq_loaded, 16 * 2 * WPARTS)
                nc.scalar.activation(wsplit[k][:, :, :, 0, :], wload[k], ACT.Copy).then_inc(w_hi, 1)
            with act.Fori(1, CHUNKS - 1) as t:
                silus(pa, t)
                copy_transposed(pa, "ln2", t - 1)
                copy_transposed(pa, "ln1", t + 1)
                mlp(t - 1)
            silus(pa, CHUNKS - 1)
            for t in range(CHUNKS - 2, CHUNKS):
                copy_transposed(pa, "ln2", t)
                mlp(t)

            def hi(kind, j, n, r):
                name, dst = f"{kind}{j}", qt if kind == "q" else kt
                act.wait_ge(stacks.sem, stacks.before("qB1", n))
                act.wait_ge(proj.sem, proj.after(name, n))
                nc.scalar.activation(dst[:, 0, j * BANK:(j + 1) * BANK], banks[:, PROJ[name], :], ACT.Identity,
                                     bias=bslot[r][:, 0:1] if kind == "q" else bslot[r][:, 1:2]).then_inc(hi_done.sem, 1)

            def lo(kind, j, n, r):
                name, dst = f"{kind}{j}", qt if kind == "q" else kt
                act.wait_ge(split.sem, split.after(name, n))
                nc.scalar.activation(dst[:, 1, j * BANK:(j + 1) * BANK], banks[:, PROJ[name], :], ACT.Identity,
                                     bias=bslot[r][:, 0:1] if kind == "q" else bslot[r][:, 1:2]).then_inc(lo_done.sem, 1)

            def values(j, n, r):
                act.wait_ge(proj.sem, proj.after(f"v{j}", n))
                nc.scalar.activation(vs[r][:, 4 * j:4 * j + 4, :], banks[:, PROJ[f"v{j}"], :].rearrange("p (m d) -> p m d", d=P),
                                     ACT.Copy).then_inc(v_done.sem, 1)

            def evacuate(c, i, r):
                act.wait_ge(pv.sem, pv.after(f"c{c}", i))
                nc.scalar.activation(attn[r][:, c, :], banks[:, ATTN[c], 0:QC + 4], ACT.Copy).then_inc(evac.sem, 1)

            def max_high(u, i):
                act.wait_ge(shifted.sem, shifted.before(f"{unit(u)}.{len(parts(u[0])) - 1}", i))
                act.wait_ge(gmax.sem, gmax.after(unit(u), i))
                nc.scalar.activation(maxrows[u][0:1, :], rowmax[u][0:1, :], ACT.Copy).then_inc(row_hi.sem, 1)

            def exps(u, i):
                c = u[0]
                act.wait_ge(pv.sem, pv.before(f"c{c}", i))
                act.wait_ge((dsum if u in DVE_SUMS else psum).sem, (dsum if u in DVE_SUMS else psum).before(unit(u), i))
                for n, (b0, b1) in enumerate(parts(c)):
                    act.wait_ge(shifted.sem, shifted.after(f"{unit(u)}.{n}", i))
                    w = min(b1 * BANK, width(c)) - b0 * BANK
                    src = banks[:, RING[u] + b0:RING[u] + b1, :].rearrange("p b n -> p (b n)")
                    nc.scalar.activation(probs[u][:, b0 * BANK:b0 * BANK + w], src[:, 0:w], ACT.Exp, scale=DH ** -0.5).then_inc(exped.sem, 1)

            def pair(i, r, carry=True, more=True):
                max_high((3, 1), i)
                if more:
                    hi("k", 0, i + 1, 1 - r)
                if carry:
                    evacuate(2, i - 1, 1 - r)
                max_high((1, 1), i)
                exps((3, 1), i)
                if more:
                    lo("k", 0, i + 1, 1 - r)
                exps((1, 1), i)
                if more:
                    hi("q", 0, i + 1, 1 - r)
                max_high((0, 0), i)
                if more:
                    lo("q", 0, i + 1, 1 - r)
                    hi("k", 1, i + 1, 1 - r)
                max_high((3, 0), i)
                if more:
                    lo("k", 1, i + 1, 1 - r)
                max_high((1, 0), i)
                exps((3, 0), i)
                if more:
                    hi("q", 1, i + 1, 1 - r)
                exps((1, 0), i)
                if more:
                    lo("q", 1, i + 1, 1 - r)
                if carry:
                    evacuate(0, i - 1, 1 - r)
                exps((0, 0), i)
                max_high((0, 1), i)
                evacuate(3, i, r)
                max_high((2, 0), i)
                exps((2, 0), i)
                max_high((2, 1), i)
                if more:
                    values(0, i + 1, 1 - r)
                exps((2, 1), i)
                exps((0, 1), i)
                if more:
                    values(1, i + 1, 1 - r)
                evacuate(1, i, r)

            hi("k", 0, 0, 0)
            lo("k", 0, 0, 0)
            hi("q", 0, 0, 0)
            lo("q", 0, 0, 0)
            hi("k", 1, 0, 0)
            lo("k", 1, 0, 0)
            hi("q", 1, 0, 0)
            lo("q", 1, 0, 0)
            values(0, 0, 0)
            values(1, 0, 0)
            pair(0, 0, carry=False)
            with act.Fori(0, TURNS // 2 - 1) as i2:
                pair(i2 * 2 + 1, 1)
                pair(i2 * 2 + 2, 0)
            pair(TURNS - 1, 1, more=False)
            evacuate(2, TURNS - 1, 1)
            evacuate(0, TURNS - 1, 1)

            copy_transposed(pd, "ln1", 0)
            with act.Fori(0, CHUNKS - 1) as t:
                silus(pd, t)
                copy_transposed(pd, "ln1", t + 1)
            silus(pd, CHUNKS - 1)

        @block.vector
        def _(dve):
            give_credits(dve, "vector")
            steps = Steps(dve, dve_step)
            nc.vector.memset(ones[:], 1.0).then_inc(consts, 1)
            nc.vector.memset(ones_row[:], 1.0).then_inc(consts, 1)
            nc.vector.memset(bvx, 1.0).then_inc(consts, 1)
            dve.wait_ge(consts, 3)
            nc.vector.tensor_scalar(minus1[:], bvx[:, 0, :], -1.0, None, ALU.mult).then_inc(consts, 1)
            for u in UNITS:
                nc.vector.tensor_scalar(maxrows[u][:, 0:P], bvx[:, 0, :], 0.0, None, ALU.mult).then_inc(consts, 1)
                nc.vector.tensor_scalar(maxrows[u][:, P:QC], bvx[:, 0, :], 0.0, None, ALU.mult).then_inc(consts, 1)
            for r in range(2):
                for h in range(2):
                    nc.vector.memset(woslot[r][half(1 - h), h, :], 0.0).then_inc(consts, 1)
            dve.wait_ge(gp_const, 4)
            nc.vector.tensor_scalar(minus_ident[:], ident[:], -1.0, None, ALU.mult).then_inc(consts, 1)
            dve.wait_ge(consts, 9 + 2 * len(UNITS))
            dve.wait_ge(ints_loaded, 16 * 3)
            nc.vector.tensor_copy(wff[:], iload[:, 0:2 * HID].rearrange("p (j n) -> p j n", n=P)).then_inc(weights_ready, 1)
            nc.vector.tensor_copy(wdn[:], iload[:, 2 * HID:3 * HID].rearrange("p (j n) -> p j n", n=P)).then_inc(weights_ready, 1)

            def statistics(t, ln, turn, at):
                dve.wait_ge(t.rstd[ln].sem, t.rstd[ln].before("r", turn))
                if ln == "ln2":
                    dve.wait_ge(t.x1.sem, t.x1.after("x", turn))
                for k in range(CT):
                    nc.vector.bn_stats(stats[ln][:, k, :], xres[:, bass.ds(at + k * D, D)]).then_inc(t.stat[ln].sem, 1)
                dve.wait_ge(t.stat[ln].sem, t.stat[ln].after(f"s{CT - 1}", turn))
                dve.sem_inc(idle, 1)
                for k in range(CT):
                    nc.vector.bn_aggr(mv[ln][:, k, :], stats[ln][:, k, :]).then_inc(t.stat[ln].sem, 1)

            def layernorm(t, ln, turn, at):
                dve.wait_ge(t.tr[ln].sem, t.tr[ln].before("t", turn))
                dve.wait_ge(t.rstd[ln].sem, t.rstd[ln].after("r", turn))
                for k in range(CT):
                    last = nc.vector.tensor_scalar(xn[ln][:, k, :], xres[:, bass.ds(at + k * D, D)], mv[ln][:, k, 0:1],
                                                   rstd[ln][:, k:k + 1], ALU.subtract, ALU.mult)
                last.then_inc(t.norm[ln].sem, 1)

            def low(t, turn):
                dve.wait_ge(t.copied["ln1"].sem, t.copied["ln1"].after("c", turn))
                nc.vector.tensor_tensor(xth[:, 1, :], banks[:, T_BANK["ln1"], :], xth[:, 0, :], ALU.subtract).then_inc(t.xlo.sem, 1)

            def gate(t, turn):
                for j in range(HB):
                    dve.wait_ge(t.silu.sem, t.silu.after(f"g{j}", turn))
                    dve.wait_ge(t.gu.sem, t.gu.after(f"u{j}", turn))
                    dve.wait_ge(t.down.sem, t.down.before("d", turn))
                    nc.vector.tensor_tensor(hidden[:, j, :], gated[:, j, :], banks[:, 1 + HB + j, :], ALU.mult).then_inc(t.hid.sem, 1)

            def residual(t, turn, at):
                dve.wait_ge(t.down.sem, t.down.after("d", turn))
                here = xres[:, bass.ds(at, CT * D)]
                nc.vector.scalar_tensor_tensor(out=here, in0=banks[:, DOWN, :], scalar=0.5 * FS * FS, in1=here,
                                               op0=ALU.mult, op1=ALU.add).then_inc(t.x1.sem, 1)

            def h_low(turn):
                dve.wait_ge(pa.hhi.sem, pa.hhi.after("h", turn))
                dve.wait_ge(pa.hstore.sem, pa.hstore.before("h", turn))
                nc.vector.scalar_tensor_tensor(out=hch[:, 1, :], in0=banks[:, T_BANK["ln2"], :], scalar=b2_sb[:], in1=hch[:, 0, :],
                                               op0=ALU.add, op1=ALU.subtract).then_inc(pa.hlo.sem, 1)

            dve.wait_ge(x_loaded, 16 * 2)
            statistics(pa, "ln1", 0, 0)
            layernorm(pa, "ln1", 0, 0)
            statistics(pa, "ln1", 1, CH)
            low(pa, 0)
            layernorm(pa, "ln1", 1, CH)
            dve.wait_ge(loaded, 16 * 8)
            for g in range(PAIRS):
                nc.vector.tensor_scalar(bvx[:, g, :], bvx[:, g, :], bv_sb[:, g:g + 1], None, ALU.mult).then_inc(bvx_ready, 1)
            gate(pa, 0)
            low(pa, 1)
            residual(pa, 0, 0)
            for k in range(WPARTS):
                dve.wait_ge(w_hi, k + 1)
                dve.wait_ge(wq_loaded, 16 * 2 * WPARTS)
                nc.vector.tensor_tensor(wsplit[k][:, :, :, 1, :], wload[k], wsplit[k][:, :, :, 0, :], ALU.subtract).then_inc(w_lo, 1)
            with dve.Fori(1, CHUNKS - 1) as t:
                at_last, at, at_next = dve.snap((t - 1) * CH), dve.snap(t * CH), dve.snap((t + 1) * CH)
                statistics(pa, "ln2", t - 1, at_last)
                statistics(pa, "ln1", t + 1, at_next)
                layernorm(pa, "ln2", t - 1, at_last)
                layernorm(pa, "ln1", t + 1, at_next)
                gate(pa, t)
                low(pa, t + 1)
                residual(pa, t, at)
                h_low(t - 1)
            t = CHUNKS - 1
            statistics(pa, "ln2", t - 1, (t - 1) * CH)
            layernorm(pa, "ln2", t - 1, (t - 1) * CH)
            gate(pa, t)
            residual(pa, t, t * CH)
            h_low(t - 1)
            statistics(pa, "ln2", t, t * CH)
            layernorm(pa, "ln2", t, t * CH)
            h_low(t)
            dve.wait_ge(pa.biased.sem, pa.biased.after("b", CHUNKS - 1))

            def block_max(u, i):
                c, acc, b0 = u[0], blockmax[u], RING[u]
                last_bank = banks[:, b0 + c, :]
                used_by(dve, gmax, MAX_ORDER, u, i)
                if c:
                    dve.wait_ge(scores.sem, scores.after(unit(u) + "a", i))
                    steps.mark(nc.vector.tensor_reduce(acc[:], banks[:, b0:b0 + c, :].rearrange("p b (s q) -> p q b s", s=2), AX.XY, ALU.max))
                dve.wait_ge(scores.sem, scores.after(unit(u) + "b", i))
                if c:
                    steps.wait()
                    steps.mark(nc.vector.tensor_tensor(acc[:], last_bank[:, 0:QC], acc[:], ALU.max))
                else:
                    steps.mark(nc.vector.tensor_copy(acc[:], last_bank[:, 0:QC]))
                partial = pieces(c)[2 * c + 1:]
                for n, (_, col, w, q0) in enumerate(partial):
                    steps.wait()
                    col -= c * BANK
                    m = nc.vector.tensor_tensor(acc[:, q0:q0 + w], last_bank[:, col:col + w], acc[:, q0:q0 + w], ALU.max)
                    if n == len(partial) - 1:
                        m.then_inc(maxed.sem, 1)
                    else:
                        steps.mark(m)

            def max_low(u, i):
                dve.wait_ge(row_hi.sem, row_hi.after(unit(u), i))
                nc.vector.tensor_tensor(maxrows[u][32:33, :], rowmax[u][0:1, :], maxrows[u][0:1, :], ALU.subtract).then_inc(rows.sem, 1)

            def key_sum(u, i):
                c, pr, acc = u[0], probs[u], keysum[u]
                dve.wait_ge(exped.sem, exped.after(f"{unit(u)}.{len(parts(c)) - 1}", i))
                dve.wait_ge(pv.sem, pv.before(f"c{c}", i))
                full = 2 * c + 1
                steps.mark(nc.vector.tensor_reduce(acc[:], pr[:, 0:full * QC].rearrange("p (s q) -> p q s", s=full), AX.X, ALU.add))
                partial = pieces(c)[full:]
                for n, (_, col, w, q0) in enumerate(partial):
                    steps.wait()
                    add = nc.vector.tensor_tensor(acc[:, q0:q0 + w], acc[:, q0:q0 + w], pr[:, col:col + w], ALU.add)
                    if n == len(partial) - 1:
                        add.then_inc(dsum.sem, 1)
                    else:
                        steps.mark(add)

            def reciprocals(c, i, r):
                dve.wait_ge(evac.sem, evac.after(f"c{c}", i))
                nc.vector.reciprocal(recips[r][:, c, :], attn[r][:, c, QC:QC + 4]).then_inc(recip.sem, 1)

            def add_output(c, i, r):
                at = (i // PAIRS) * N + c * QC
                at = at if isinstance(at, int) else dve.snap(at)
                dve.wait_ge(wo_added.sem, wo_added.before(f"o{c}", i))
                dve.wait_ge(recip.sem, recip.after(f"c{c}", i))
                dve.wait_ge(wo_done.sem, wo_done.after(f"o{c}", i))
                for h in range(2):
                    if h:
                        steps.wait()
                    for b in range(2):
                        here = xres[:, bass.ds(at + b * P, P)]
                        k = 2 * b + h
                        add = nc.vector.scalar_tensor_tensor(out=here, in0=banks[:, OUT[f"o{c}"], k * P:(k + 1) * P], scalar=recips[r][:, c, k:k + 1],
                                                             in1=here, op0=ALU.mult, op1=ALU.add)
                        if h == 0:
                            steps.mark(add)
                add.then_inc(wo_added.sem, 1)

            def pair(i, r, carry=True, more=True):
                steps.begin(i)
                block_max((3, 1), i)
                block_max((1, 1), i)
                max_low((3, 1), i)
                max_low((1, 1), i)
                block_max((0, 0), i)
                block_max((3, 0), i)
                block_max((1, 0), i)
                max_low((0, 0), i)
                max_low((3, 0), i)
                key_sum((1, 1), i)
                max_low((1, 0), i)
                key_sum((3, 0), i)
                if carry:
                    add_output(3, i - 1, 1 - r)
                block_max((0, 1), i)
                if carry:
                    add_output(1, i - 1, 1 - r)
                block_max((2, 0), i)
                max_low((2, 0), i)
                block_max((2, 1), i)
                max_low((0, 1), i)
                max_low((2, 1), i)
                if carry:
                    reciprocals(0, i - 1, 1 - r)
                    reciprocals(2, i - 1, 1 - r)
                    add_output(0, i - 1, 1 - r)
                    add_output(2, i - 1, 1 - r)
                key_sum((2, 0), i)
                reciprocals(3, i, r)
                reciprocals(1, i, r)
                steps.end()


            pair(0, 0, carry=False)
            with dve.Fori(0, TURNS // 2 - 1) as i2:
                pair(i2 * 2 + 1, 1)
                pair(i2 * 2 + 2, 0)
            pair(TURNS - 1, 1, more=False)
            steps.begin(TURNS)
            add_output(3, TURNS - 1, 1)
            add_output(1, TURNS - 1, 1)
            reciprocals(0, TURNS - 1, 1)
            reciprocals(2, TURNS - 1, 1)
            add_output(0, TURNS - 1, 1)
            add_output(2, TURNS - 1, 1)

            dve.wait_ge(wo_added.sem, wo_added.after("o2", TURNS - 1))
            statistics(pd, "ln1", 0, 0)
            layernorm(pd, "ln1", 0, 0)
            low(pd, 0)
            with dve.Fori(0, CHUNKS - 1) as t:
                at, at_next = dve.snap(t * CH), dve.snap((t + 1) * CH)
                statistics(pd, "ln1", t + 1, at_next)
                layernorm(pd, "ln1", t + 1, at_next)
                gate(pd, t)
                low(pd, t + 1)
                residual(pd, t, at)
            gate(pd, CHUNKS - 1)
            residual(pd, CHUNKS - 1, (CHUNKS - 1) * CH)

        @block.tensor
        def _(pe):
            give_credits(pe, "tensor")
            mm = nc.tensor.matmul

            def transposed(t, ln, turn):
                pe.wait_ge(t.norm[ln].sem, t.norm[ln].after("n", turn))
                for k in range(CT):
                    last = nc.tensor.transpose(banks[:, T_BANK[ln], k * P:(k + 1) * P], xn[ln][:, k, :], ident[:])
                last.then_inc(t.tr[ln].sem, 1)

            def gate_up(t, turn):
                pe.wait_ge(t.xlo.sem, t.xlo.after("l", turn))
                for j in range(2 * HB):
                    if j < HB:
                        pe.wait_ge(t.silu.sem, t.silu.before(f"g{j}", turn))
                    else:
                        pe.wait_ge(t.hid.sem, t.hid.before(f"h{j - HB}", turn))
                    mm(banks[:, 1 + j, :], wff[:, j, :], xth[:, 0, :], start=True, stop=False)
                    mm(banks[:, 1 + j, :], wff[:, j, :], xth[:, 1, :], start=False, stop=True).then_inc(t.gu.sem, 1)

            def down(t, turn):
                pe.wait_ge(t.hid.sem, t.hid.after(f"h{HB - 1}", turn))
                pe.wait_ge(t.x1.sem, t.x1.before("x", turn))
                for k in range(CT):
                    for j in range(HB):
                        last = mm(banks[:, DOWN, k * P:(k + 1) * P], hidden[:, j, k * P:(k + 1) * P], wdn[:, j, :],
                                  start=(j == 0), stop=(j == HB - 1))
                last.then_inc(t.down.sem, 1)

            def mlp1(turn):
                pe.wait_ge(pa.copied["ln2"].sem, pa.copied["ln2"].after("c", turn))
                mm(banks[:, T_BANK["ln2"], :], w1_sb[:], x2t, start=True, stop=True).then_inc(pa.m1.sem, 1)

            def mlp2(turn):
                pe.wait_ge(pa.y1.sem, pa.y1.after("y", turn))
                mm(banks[:, T_BANK["ln2"], :], w2_sb[:], y1, start=True, stop=True).then_inc(pa.m2.sem, 1)

            pe.wait_ge(gp_const, 6)
            transposed(pa, "ln1", 0)
            pe.wait_ge(weights_ready, 2)
            gate_up(pa, 0)
            pe.wait_ge(pa.silu.sem, pa.silu.after("g0", 0))
            transposed(pa, "ln1", 1)
            pe.wait_ge(loaded, 16 * 8)
            pe.wait_ge(bvx_ready, PAIRS)
            for g in range(PAIRS):
                mm(banks[:, WORK, 0:P], bvx[:, g, :], wo_sb[:, g, :], start=(g == 0), stop=False)
            mm(banks[:, WORK, 0:P], ones_row[:], bo_row[:], start=False, stop=True).then_inc(bo_done, 1)
            down(pa, 0)
            pe.wait_ge(bo_done, 2)
            with pe.Fori(1, CHUNKS - 1) as t:
                gate_up(pa, t)
                pe.wait_ge(pa.hlo.sem, pa.hlo.before("h", t - 1))
                transposed(pa, "ln2", t - 1)
                mlp1(t - 1)
                pe.wait_ge(pa.silu.sem, pa.silu.after("g0", t))
                transposed(pa, "ln1", t + 1)
                down(pa, t)
                mlp2(t - 1)
            t = CHUNKS - 1
            gate_up(pa, t)
            pe.wait_ge(pa.hlo.sem, pa.hlo.before("h", t - 1))
            transposed(pa, "ln2", t - 1)
            mlp1(t - 1)
            down(pa, t)
            mlp2(t - 1)
            pe.wait_ge(pa.hlo.sem, pa.hlo.before("h", t))
            transposed(pa, "ln2", t)
            mlp1(t)
            mlp2(t)
            pe.wait_ge(consts, 9 + 2 * len(UNITS))

            def read_by(step, turn):
                if step[0] == "c":
                    pe.wait_ge(evac.sem, evac.after(step, turn))
                elif step[0] == "o":
                    pe.wait_ge(wo_added.sem, wo_added.after(step, turn))
                elif step[0] == "v":
                    pe.wait_ge(v_done.sem, v_done.after(step, turn))
                elif step[0] in "kq":
                    pe.wait_ge(lo_done.sem, lo_done.after(step, turn))
                else:
                    pe.wait_ge(exped.sem, exped.after(step, turn))

            def subtract_high(name, n):
                kind, j = name[0], int(name[1])
                pe.wait_ge(hi_done.sem, hi_done.after(name, n))
                mm(banks[:, PROJ[name], :], minus_ident[:], (qt if kind == "q" else kt)[:, 0, j * BANK:(j + 1) * BANK],
                   start=False, stop=True, skip_group_check=True).then_inc(split.sem, 1)

            def freed(bank, step, i):
                order = BANK_ORDER[bank]
                k = [name for name, _ in order].index(step)
                for back in range(1, 2 * len(order)):
                    name, lag = order[(k - back) % len(order)]
                    at = i + (k - back) // len(order)
                    if isinstance(at, int) and (at < -1 or (at - lag < 0) or (at - lag >= TURNS)):
                        continue
                    if name[0] in "0123":
                        u = (int(name[0]), "AB".index(name[1]))
                        name = f"{name}.{(bank - RING[u]) // 2}"
                    read_by(name, at - lag)
                    if isinstance(at, int) or lag <= 0 or (k >= back and not (k - back) // len(order)):
                        return

            def project(name, n, r, i):
                kind, j = name[0], int(name[1])
                if name == "k0":
                    pe.wait_ge(slots.sem, slots.after("b", n))
                freed(PROJ[name], name, i)
                bank = banks[:, PROJ[name], :]
                w = wslot[r][:, "qkv".index(kind)]
                if kind != "v":
                    toks = slice(j * BANK, (j + 1) * BANK)
                    mm(bank, w[:, 0, :], hb[r][:, 0, toks], start=True, stop=False)
                    mm(bank, w[:, 0, :], hb[r][:, 1, toks], start=False, stop=False)
                    last = mm(bank, w[:, 1, :], hb[r][:, 0, toks], start=False, stop=True)
                else:
                    for m in range(4):
                        toks = slice((4 * j + m) * P, (4 * j + m + 1) * P)
                        dst = bank[:, m * P:(m + 1) * P]
                        mm(dst, hb[r][:, 0, toks], w[:, 0, :], start=True, stop=False)
                        mm(dst, hb[r][:, 0, toks], w[:, 1, :], start=False, stop=False)
                        last = mm(dst, hb[r][:, 1, toks], w[:, 0, :], start=False, stop=True)
                last.then_inc(proj.sem, 1)

            def score(u, i, r):
                c, h = u
                if u == UNITS[0]:
                    pe.wait_ge(stacks.sem, stacks.after("qB1", i))
                for kb, col, w, q0 in pieces(c):
                    b = col // BANK
                    first = col % BANK == 0
                    if first:
                        if b == c and c:
                            last.then_inc(scores.sem, 1)
                        freed(RING[u] + b, unit(u), i)
                    dst = banks[:, RING[u] + b, col % BANK:col % BANK + w]
                    qcols = slice(c * QC + q0, c * QC + q0 + w)
                    m0 = c * QC + q0 - (kb * P - WINDOW)
                    edge = min(P - m0, w) if m0 < P else 0
                    mm(dst, ks[r][h][:, 0, kb * P:(kb + 1) * P], qs[r][h][:, qcols], start=first, stop=False, skip_group_check=True)
                    last = mm(dst, ks[r][h][:, 1, kb * P:(kb + 1) * P], qs[r][h][:, qcols], start=False, stop=not edge, skip_group_check=True)
                    if edge:
                        last = mm(dst[:, 0:edge], ident16[:], mask16[:, m0:m0 + edge], start=False, stop=True, skip_group_check=True)
                last.then_inc(scores.sem, 1)

            def shift(u, i):
                c = u[0]
                pe.wait_ge(rows.sem, rows.after(unit(u), i))
                for b0, b1 in parts(c):
                    for b in range(b0, b1):
                        bank = banks[:, RING[u] + b, :]
                        here = [(col - b * BANK, w, q0) for _, col, w, q0 in pieces(c) if col // BANK == b]
                        if len(here) == 2 and here[1][1] == QC:
                            last = mm(bank.rearrange("p (s q) -> p s q", s=2), minus1[:], maxrows[u][:].unsqueeze(1).to_broadcast([P, 2, QC]),
                                      start=False, stop=True, skip_group_check=True)
                        else:
                            for col, w, q0 in here:
                                last = mm(bank[:, col:col + w], minus1[:], maxrows[u][:, q0:q0 + w], start=False, stop=True, skip_group_check=True)
                    last.then_inc(shifted.sem, 1)

            def attend(c, i, r, now):
                freed(ATTN[c], f"c{c}", now)
                if c == CORDER[0]:
                    pe.wait_ge(v_done.sem, v_done.after("v1", i))
                pe.sem_inc(idle, 1)
                end = max((f"{c}{h}.{len(parts(c)) - 1}" for h in "AB"), key=exped.events.index)
                pe.wait_ge(exped.sem, exped.after(end, i))
                ps = pieces(c)
                for kb, col, w, q0 in ps:
                    for h in range(2):
                        mm(banks[half(h), ATTN[c], q0:q0 + w], vs[r][:, kb, half(h)], probs[c, h][:, col:col + w],
                           start=(kb == 0), stop=(kb == ps[-1][0]), skip_group_check=True)
                for h in range(2):
                    pe.wait_ge((dsum if (c, h) in DVE_SUMS else psum).sem, (dsum if (c, h) in DVE_SUMS else psum).after(unit((c, h)), i))
                    for b in range(2):
                        k = QC + 2 * b + h
                        last = mm(banks[:, ATTN[c], k:k + 1], keysum[c, h][:, b * P:(b + 1) * P], ones[:], start=True, stop=True, skip_group_check=True)
                last.then_inc(pv.sem, 1)

            def output(c, i, r, now):
                if c == 3:
                    pe.wait_ge(woslots[r].sem, woslots[r].after("wB", i // 2))
                freed(OUT[f"o{c}"], f"o{c}", now)
                pe.sem_inc(idle, 1)
                pe.wait_ge(evac.sem, evac.after(f"c{c}", i))
                for b in range(2):
                    last = mm(banks[:, OUT[f"o{c}"], 2 * b * P:2 * (b + 1) * P], attn[r][:, c, b * P:(b + 1) * P],
                              woslot[r][:].rearrange("p h n -> p (h n)"), start=True, stop=True)
                last.then_inc(wo_done.sem, 1)

            def pair(i, r, carry=True, more=True):
                score((3, 1), i, r)
                score((1, 1), i, r)
                if more:
                    project("k0", i + 1, 1 - r, i)
                if carry:
                    attend(2, i - 1, 1 - r, i)
                shift((3, 1), i)
                score((0, 0), i, r)
                shift((1, 1), i)
                if more:
                    subtract_high("k0", i + 1)
                score((3, 0), i, r)
                if more:
                    project("q0", i + 1, 1 - r, i)
                score((1, 0), i, r)
                if more:
                    subtract_high("q0", i + 1)
                    project("k1", i + 1, 1 - r, i)
                shift((0, 0), i)
                if more:
                    subtract_high("k1", i + 1)
                shift((3, 0), i)
                if carry:
                    output(3, i - 1, 1 - r, i)
                shift((1, 0), i)
                if carry:
                    output(1, i - 1, 1 - r, i)
                if more:
                    project("q1", i + 1, 1 - r, i)
                score((0, 1), i, r)
                if carry:
                    attend(0, i - 1, 1 - r, i)
                if more:
                    subtract_high("q1", i + 1)
                score((2, 0), i, r)
                attend(3, i, r, i)
                score((2, 1), i, r)
                shift((2, 0), i)
                if carry:
                    output(0, i - 1, 1 - r, i)
                if more:
                    project("v0", i + 1, 1 - r, i)
                if carry:
                    output(2, i - 1, 1 - r, i)
                shift((0, 1), i)
                if more:
                    project("v1", i + 1, 1 - r, i)
                shift((2, 1), i)
                attend(1, i, r, i)

            pe.wait_ge(pa.hlo.sem, pa.hlo.after("h", CHUNKS - 1))
            pe.wait_ge(pa.x1.sem, pa.x1.after("x", CHUNKS - 1))
            project("k0", 0, 0, -1)
            subtract_high("k0", 0)
            project("q0", 0, 0, -1)
            subtract_high("q0", 0)
            project("k1", 0, 0, -1)
            subtract_high("k1", 0)
            project("q1", 0, 0, -1)
            subtract_high("q1", 0)
            project("v0", 0, 0, -1)
            project("v1", 0, 0, -1)
            pair(0, 0, carry=False)
            with pe.Fori(0, TURNS // 2 - 1) as i2:
                pair(i2 * 2 + 1, 1)
                pair(i2 * 2 + 2, 0)
            pair(TURNS - 1, 1, more=False)
            attend(2, TURNS - 1, 1, TURNS)
            output(3, TURNS - 1, 1, TURNS)
            output(1, TURNS - 1, 1, TURNS)
            attend(0, TURNS - 1, 1, TURNS)
            output(0, TURNS - 1, 1, TURNS)
            output(2, TURNS - 1, 1, TURNS)

            pe.wait_ge(wo_added.sem, wo_added.after("o2", TURNS - 1))
            transposed(pd, "ln1", 0)
            with pe.Fori(0, CHUNKS - 1) as t:
                gate_up(pd, t)
                pe.wait_ge(pd.silu.sem, pd.silu.after("g0", t))
                transposed(pd, "ln1", t + 1)
                down(pd, t)
            gate_up(pd, CHUNKS - 1)
            down(pd, CHUNKS - 1)


def kernel(L0_attn_x, L0_attn_W1, L0_attn_b1, L0_attn_W2, L0_attn_b2, L0_attn_Wg, L0_attn_bg, L0_attn_Wo, L0_attn_bo,
           L0_ffn_w_gate, L0_ffn_w_up, L0_ffn_w_down):
    import numpy as np
    import concourse.bacc as bacc
    from concourse.bass_utils import run_bass_kernel_spmd

    x = np.asarray(L0_attn_x)
    bg = np.asarray(L0_attn_bg).reshape(3, -1, P)
    arrays = {
        "x": x.reshape(-1, x.shape[-1]),
        "w1t": np.asarray(L0_attn_W1).T, "b1": np.asarray(L0_attn_b1).reshape(-1, 1),
        "w2t": np.asarray(L0_attn_W2).T, "b2": np.asarray(L0_attn_b2).reshape(-1, 1),
        "wqkvt": np.asarray(L0_attn_Wg).T,
        "bqk": bg[0:2].transpose(2, 1, 0).reshape(P, -1), "bv": bg[2].T,
        "wot": np.asarray(L0_attn_Wo).T, "bo": np.asarray(L0_attn_bo).reshape(1, -1),
        "wgatet": np.asarray(L0_ffn_w_gate).T, "wupt": np.asarray(L0_ffn_w_up).T, "wdownt": np.asarray(L0_ffn_w_down).T,
    }
    nc = bacc.Bacc("TRN2", target_bir_lowering=False, num_devices=1)
    feed, args = {}, []
    for name, a in arrays.items():
        feed[f"in_{name}"] = np.ascontiguousarray(a)
        args.append(nc.dram_tensor(f"in_{name}", a.shape, mybir.dt.from_np(a.dtype), kind="ExternalInput").ap())
    out = nc.dram_tensor("y", arrays["x"].shape, F32, kind="ExternalOutput").ap()
    macaron(nc, *args, out)
    r = run_bass_kernel_spmd(nc, [feed], core_ids=[0])
    return r.results[0]["y"].reshape(x.shape)
```
